# Optimizing a Trainium2 kernel written in Bass

```python
import numpy as np
import jax
import jax.numpy as jnp

def _softmax(x, axis=-1):
    return jax.nn.softmax(x, axis=axis)

def _gelu(x):
    return jax.nn.gelu(x, approximate=True)

def _silu(x):
    return jax.nn.silu(x)

def _sigmoid(x):
    return jax.nn.sigmoid(x)

def _layernorm(x, axis=-1, eps=1e-05):
    m = jnp.mean(x, axis=axis, keepdims=True)
    v = jnp.var(x, axis=axis, keepdims=True)
    return (x - m) / jnp.sqrt(v + eps)

def _scatter_add(tgt, idx, src, axis=0):
    return tgt.at[idx].add(src)

def _segment_sum(src, seg, n):
    return jax.ops.segment_sum(src, seg, n)
kernel_name = 'mk_gnn_preln_d1_gnn_r32_94dba9'

def setup_inputs(seed: int=0):
    np.random.seed(seed)
    _w = jnp.asarray

    def _rec_inputs():
        import jax
        import jax.numpy as jnp
        _gk = jax.random.key(seed)
        x = -0.000125 + 0.9999 * jax.random.normal(jax.random.fold_in(_gk, 1), (2048, 512), jnp.float32)
        _s = jax.random.randint(jax.random.fold_in(_gk, 2), (16384,), 0, 2048, jnp.int32)
        _d = jax.random.randint(jax.random.fold_in(_gk, 3), (16384,), 0, 2048, jnp.int32)
        _loop = jnp.arange(2048, dtype=jnp.int32)
        src = jnp.concatenate([_s, _d, _loop])
        dst = jnp.concatenate([_d, _s, _loop])
        _o = jnp.argsort(dst, stable=True)
        src = src[_o]
        dst = dst[_o]
        return (x, src, dst)
    x, src, dst = _rec_inputs()

    def _L0_gnn_setup():
        import jax, jax.numpy as jnp
        import numpy as np
        N = 2048
        F = 512
        H = 512
        E = 16384
        key = jax.random.key(seed)
        ks = jax.random.split(key, 12)
        s = 0.02
        return {'x': jax.random.normal(ks[0], (N, F), dtype=jnp.float32), 'edge_index': jax.random.randint(ks[1], (2, E), 0, N, dtype=jnp.int64), 'W_rel1': jax.random.normal(ks[2], (H, F), dtype=jnp.float32) * s, 'b_rel1': jnp.zeros((H,), dtype=jnp.float32), 'W_root1': jax.random.normal(ks[3], (H, F), dtype=jnp.float32) * s, 'W_lin1': jax.random.normal(ks[4], (H, H), dtype=jnp.float32) * s, 'b_lin1': jnp.zeros((H,), dtype=jnp.float32), 'W_rel2': jax.random.normal(ks[5], (H, H), dtype=jnp.float32) * s, 'b_rel2': jnp.zeros((H,), dtype=jnp.float32), 'W_root2': jax.random.normal(ks[6], (H, H), dtype=jnp.float32) * s, 'W_lin2': jax.random.normal(ks[7], (H, H), dtype=jnp.float32) * s, 'b_lin2': jnp.zeros((H,), dtype=jnp.float32)}
    _L0_gnn_all = _L0_gnn_setup()
    _L0_gnn_in = {k: v for k, v in _L0_gnn_all.items() if k in ('W_rel1', 'b_rel1', 'W_root1', 'W_lin1', 'b_lin1', 'W_rel2', 'b_rel2', 'W_root2', 'W_lin2', 'b_lin2')}
    del _L0_gnn_all
    return {'x': x, 'src': src, 'dst': dst, 'L0_gnn_W_rel1': _L0_gnn_in['W_rel1'], 'L0_gnn_b_rel1': _L0_gnn_in['b_rel1'], 'L0_gnn_W_root1': _L0_gnn_in['W_root1'], 'L0_gnn_W_lin1': _L0_gnn_in['W_lin1'], 'L0_gnn_b_lin1': _L0_gnn_in['b_lin1'], 'L0_gnn_W_rel2': _L0_gnn_in['W_rel2'], 'L0_gnn_b_rel2': _L0_gnn_in['b_rel2'], 'L0_gnn_W_root2': _L0_gnn_in['W_root2'], 'L0_gnn_W_lin2': _L0_gnn_in['W_lin2'], 'L0_gnn_b_lin2': _L0_gnn_in['b_lin2']}

def reference(x, src, dst, L0_gnn_W_rel1, L0_gnn_b_rel1, L0_gnn_W_root1, L0_gnn_W_lin1, L0_gnn_b_lin1, L0_gnn_W_rel2, L0_gnn_b_rel2, L0_gnn_W_root2, L0_gnn_W_lin2, L0_gnn_b_lin2):
    import jax
    import jax.numpy as jnp

    def _L0_gnn_ref(x, edge_index, W_rel1, b_rel1, W_root1, W_lin1, b_lin1, W_rel2, b_rel2, W_root2, W_lin2, b_lin2):
        import jax, jax.numpy as jnp
        import numpy as np
        N = 2048
        F = 512
        H = 512
        E = 16384
        src, dst = (edge_index[0], edge_index[1])

        def graph_conv(h, W_rel, b_rel, W_root):
            agg = jax.ops.segment_sum(h[src], dst, num_segments=N)
            return agg @ W_rel.T + b_rel + h @ W_root.T
        h = jax.nn.relu(graph_conv(x, W_rel1, b_rel1, W_root1) @ W_lin1.T + b_lin1)
        h = jax.nn.relu(graph_conv(h, W_rel2, b_rel2, W_root2) @ W_lin2.T + b_lin2)
        return h
    edge_index = jnp.stack([src, dst])
    h = jnp.maximum(_layernorm(x, axis=-1), 0.0)
    x = x + _L0_gnn_ref(h, edge_index, L0_gnn_W_rel1, L0_gnn_b_rel1, L0_gnn_W_root1, L0_gnn_W_lin1, L0_gnn_b_lin1, L0_gnn_W_rel2, L0_gnn_b_rel2, L0_gnn_W_root2, L0_gnn_W_lin2, L0_gnn_b_lin2)
    return x

_drawn_inputs = setup_inputs


def setup_inputs(seed=0):
    import zlib

    import numpy as np

    out = dict(_drawn_inputs(seed))
    spreads = {'L0_gnn_b_rel1': (0.0, 0.293),
     'L0_gnn_b_lin1': (0.0, 0.1),
     'L0_gnn_b_rel2': (0.0, 0.646),
     'L0_gnn_b_lin2': (0.0, 0.307)}
    factors = {}
    for name, (base, spread) in spreads.items():
        noise = np.random.default_rng([zlib.crc32(name.encode()), seed]).standard_normal(out[name].shape)
        drawn = base * np.exp(spread * noise) if base else spread * noise
        out[name] = jnp.asarray(drawn.astype(out[name].dtype))
    for name, factor in factors.items():
        out[name] = (out[name] * factor).astype(out[name].dtype)
    return out
```

```python
import numpy as np
import concourse.bass as bass
from concourse import mybir
from contextlib import ExitStack


def gnn_block_kernel(nc, x, src, dst, W_rel1, b_rel1, W_root1, W_lin1, b_lin1,
                     W_rel2, b_rel2, W_root2, W_lin2, b_lin2, out):
    f32, f16 = mybir.dt.float32, mybir.dt.float16
    i32, u32 = mybir.dt.int32, mybir.dt.uint32
    ALU = mybir.AluOpType
    ACT = mybir.ActivationFunctionType
    X = mybir.AxisListType.X
    ds = bass.ds

    P = 128
    N, F = x.shape
    E = src.shape[0]
    T = N // P
    K = F // P
    B = 4
    TB = T // B
    NB = N // B
    WIN = N // P
    WT = P // WIN
    HI = N // P
    KEY = HI * WIN
    CH = 3
    CAP = CH * P
    EC = E // P
    OH = P + KEY
    HB = 8
    FAR = 4096.0
    EPS = 1e-5
    SH = 16.0
    REL, ROOT, LIN, LINT = range(4)
    assert N == WIN * P and HI * WIN == KEY and E == EC * P and KEY == 256 and EC % HB == 0

    at2_dram = nc.dram_tensor("at2", (T, P, HI * P), f16, kind="Internal").ap()
    x_t = x.rearrange("(t p) f -> t p f", p=P)
    x_p = x.rearrange("(t p) f -> p t f", p=P)
    out_p = out.rearrange("(t p) f -> p t f", p=P)

    ctx = ExitStack()
    with ctx:
        def sb(name, shape, dt):
            return ctx.enter_context(nc.sbuf_tensor(name, shape, dt))

        def sem(name):
            return ctx.enter_context(nc.semaphore(name))

        At = sb("At", [P, T * HI * P], f16)
        A4 = At[:, :].rearrange("p (t s d) -> p t s d", t=T, s=HI)
        Yt = sb("Yt", [P, T * 2 * F], f16)
        Y4 = Yt[:, :].rearrange("p (t a f) -> p t a f", t=T, a=2)
        Ht = sb("Ht", [P, (B + 1) * TB * 2 * K * P], f16)
        H5 = Ht[:, :].rearrange("p (t a k n) -> p t a k n", a=2, k=K, n=P)
        Hf = Ht[:, :].bitcast(f32)
        H1 = Hf.rearrange("p (b k n) -> p b k n", b=B + 1, k=K)
        Wb = sb("Wb", [P, 2, 2, 2, K, F], f16)
        ring = sb("ring", [P, WT * CH * OH], f16)
        R4 = ring[:, :].rearrange("p (u j c) -> p u j c", u=WT, j=CH)
        xb = sb("xb", [P, 3, F], f32)
        hs = sb("hs", [P, 2, 2, F], f16)
        bias2 = sb("bias2", [P, F], f32)
        ident = sb("ident", [P, P], f32)
        ident16 = sb("ident16", [P, P], f16)
        ones = sb("ones", [P, P], f32)
        iota16 = sb("iota16", [P, KEY], f16)
        keyT = sb("keyT", [P, 2 * CH, P], f32)
        cur = sb("cur", [P, 2 * CH, WT], f32)
        delta = sb("delta", [P, HB, 8], f32)
        small = sb("small", [P, 96], f32)
        smi = sb("smi", [P, 16], i32)
        st6 = sb("st6", [P, 6], f32)
        brow = sb("brow", [1, F], f32)
        bcol = sb("bcol", [P, K, P], f32)

        raw = [Yt[:, :].bitcast(f32).rearrange("p (w k f) -> p w k f", w=4, k=K),
               At[:, T * HI * P // 2:].bitcast(f32).rearrange("p (w k f) -> p w k f", w=4, k=K)]
        Wf = At[:, 0:4 * 2 * K * F].bitcast(f32).rearrange("p (l t f) -> p l t f", l=2, t=2 * K)

        def part(base, at, n, dt):
            v = base[:, at:at + n]
            return v if dt == f32 else v.bitcast(dt)

        srcw, dstw, rel, bad, key = [part(Hf, i * CAP, CAP, dt) for i, dt in enumerate((i32, i32, f32, f32, f32))]
        SL = TB * K * P
        oh1 = Hf[:, 3 * SL:3 * SL + EC * 8].bitcast(f16).rearrange("p (c v) -> p c v", v=16)
        oh0 = Hf[:, 3 * SL + EC * 8:3 * SL + EC * 12].bitcast(f16).rearrange("p (c v) -> p c v", v=8)
        rf = ring[:, :].bitcast(f32)
        before = rf[:, 0:8 * P].rearrange("p (b w) -> p b w", b=8)
        wminus = rf[:, 8 * P:16 * P].rearrange("p (b w) -> p b w", b=8)
        dnat, bit1, bit0 = [part(rf, 16 * P + i * EC, EC, i32) for i in range(3)]
        o = 16 * P + 3 * EC
        lowi, highi, low = part(rf, o, CAP, i32), part(rf, o + CAP, CAP, i32), part(rf, o + 2 * CAP, CAP, f32)
        masked = key[:, 0:HB * 8].rearrange("p (c b) -> p c b", c=HB)

        s_src, s_dst, s_low, s_high, s_rel, s_key, s_tmp = [
            part(Hf, i * EC, EC, dt) for i, dt in enumerate((i32, i32, f32, i32, f32, f32, f32))]
        s_lowi = s_tmp.bitcast(i32)
        s_oh = [ring[:, i * OH:(i + 1) * OH] for i in range(2)]
        A2s = ring[:, 2 * OH:2 * OH + HI * P].rearrange("p (s d) -> p s d", s=HI)
        A2 = ring[:, 0:TB * HI * P].rearrange("p (t s d) -> p t s d", t=TB, s=HI)

        ho = [hs[:, j].rearrange("p a f -> p (a f)").bitcast(f32) for j in range(2)]

        at = [0]

        def col(n):
            at[0] += n
            return small[:, at[0] - n:at[0]]

        hist, wbase, b1off = col(8), col(1), col(1)
        badsum, mv, sd, rs, nb, epsc = col(1), col(2), col(1), col(2), col(2), col(1)
        wmax, wtop, wall, brel, blin, bias1 = col(2 * K), col(1), col(1), col(2 * K), col(K), col(K)
        sW = [col(1), col(1)]
        iW = [col(1), col(1)]
        hmax, htop, hall, sHs, iH, iS1, iS2 = col(B * K), col(1), col(1), col(1), col(1), col(1), col(1)
        start, pint, flag, ebits, pidx = smi[:, 0:1], smi[:, 1:2], smi[:, 2:3], smi[:, 3:4], smi[:, 4:5]

        ps = [ctx.enter_context(nc.psum_tensor(f"ps{i}", [P, F], f32)) for i in range(8)]
        ACC = (0, 1)
        TP = 2
        GY = (3, 4)
        FOLD = (5, 6)
        MISC = 7
        GZ = (0, 1, 5, 6)
        WTB = (3, 4, 0, 1)
        tp16 = ps[TP][:, :].bitcast(f16).rearrange("p (a k n) -> p a k n", a=2, k=K)

        dst_in, brow_in, b_in = sem("dst_in"), sem("brow_in"), sem("b_in")
        w_in = [[sem(f"w_in{l}{w}") for w in range(3)] for l in range(2)]
        x_in = [sem(f"x_in{i}") for i in range(3)]
        src_g, dst_g = sem("src_gathered"), sem("dst_gathered")
        consts, epsd = sem("consts"), sem("eps_set")
        pool_chain, dve_chain = sem("pool_chain"), sem("dve_chain")
        wt_done, wt_copied = sem("wt_done"), sem("wt_copied")
        fold_done, fold_copied = sem("fold_done"), sem("fold_copied")
        oh_hist, hist_done, hist_ready, start_done, start_ready = [
            sem(n) for n in ("hist_onehots", "hist_done", "hist_ready", "start_done", "start_ready")]
        keys_ready, keyT_done, cover_done, flag_set = [sem(n) for n in ("keys_ready", "keyT_done", "cover_done", "flag_set")]
        hmax_part = sem("hmax_part")
        keyT_copied = sem("keyT_copied")
        var_ready, sd_ready, norm_ready = sem("var_ready"), sem("sd_ready"), sem("norm_ready")
        h_hi, h_f32, h_lo = sem("h_hi"), sem("h_f32"), sem("h_lo")
        tp_done, hT_ready = sem("tp_done"), sem("hT_ready")
        wmax_ready, wall_ready, sW_ready, w_hi, w_lo = [sem(n) for n in ("wmax_ready", "wall_ready", "sW_ready", "w_hi", "w_lo")]
        b1_done, b1_ready, bcol_ready, b2_done, b2_ready = [sem(n) for n in ("b1_done", "b1_ready", "bcol_ready", "b2_done", "b2_ready")]
        cur_ready, onehot_ready, win_done = sem("cur_ready"), sem("onehot_ready"), sem("win_done")
        A_ready = sem("A_ready")
        y_done, y_hi, y_lo = sem("y_done"), sem("y_hi"), sem("y_lo")
        z1_done, h1_ready, hmax_ready, hall_ready, sH_ready = [
            sem(n) for n in ("z1_done", "h1_ready", "hmax_ready", "hall_ready", "sH_ready")]
        c_hi, c_lo = sem("c_hi"), sem("c_lo")
        y2_done, y2_hi, y2_lo = sem("y2_done"), sem("y2_hi"), sem("y2_lo")
        z2_done, z2_read, o_ready = sem("z2_done"), sem("z2_read"), sem("o_ready")
        xr_in = [sem(f"xr_in{i}") for i in range(2)]
        o_out = [sem(f"o_out{i}") for i in range(2)]
        sl_in, sl_oh, sl_free, sl_win, sl_A, sl_A2, sl_st, sl_chain = [
            sem(n) for n in ("slow_in", "slow_onehot", "slow_free", "slow_window", "slow_A", "slow_A2", "slow_stored", "slow_chain")]
        a2_in, a2_used = sem("a2_in"), sem("a2_used")

        block = ctx.enter_context(nc.Block())

        @block.sync
        def _(sp):
            W = ((W_rel1, W_root1, W_lin1), (W_rel2, W_root2, W_lin2))

            def load_w(l, w):
                sp.dma_start(raw[l][:, w], W[l][w].rearrange("(k p) f -> p k f", p=P)).then_inc(w_in[l][w], 16)

            def load_x(t):
                if t >= 3:
                    sp.wait_ge(h_lo, t - 2)
                sp.dma_start(xb[:, t % 3, :], x_t[t]).then_inc(x_in[t % 3], 16)

            sp.dma_start(dnat, dst.rearrange("(p c) -> p c", p=P)).then_inc(dst_in, 16)
            load_w(0, LIN)
            load_w(0, REL)
            load_x(0)
            load_x(1)
            load_x(2)
            load_w(0, ROOT)
            sp.dma_start(brow[:, :], b_lin2.rearrange("(a f) -> a f", a=1)).then_inc(brow_in, 16)
            for v, d in ((brel[:, 0:K], b_rel1), (brel[:, K:2 * K], b_rel2), (blin, b_lin1)):
                sp.dma_start(v, d.rearrange("(k p) -> p k", p=P), allow_slow_non_contiguous=True).then_inc(b_in, 16)
            load_x(3)
            load_w(1, LIN)
            load_w(1, REL)
            load_w(1, ROOT)
            for t in range(4, T):
                load_x(t)

            sp.sem_inc(sl_st, 16)
            sp.wait_ge(flag_set, 1)
            slow = sp.value_load(flag[0:1, 0:1], min_val=0, max_val=1)
            with sp.If(slow == 1):
                sp.wait_ge(A_ready, T * WT // 2 + 2)
                sp.dma_start(s_src, src.rearrange("(p c) -> p c", p=P)).then_inc(sl_in, 16)
                sp.dma_start(s_dst, dst.rearrange("(p c) -> p c", p=P)).then_inc(sl_in, 16)
                with sp.Fori(0, T) as i:
                    sp.wait_ge(sl_A2, (i + 1) * WT + 1)
                    sp.dma_start(at2_dram[ds(i, 1)].rearrange("o p n -> (o p) n"),
                                 A2s.rearrange("p s d -> p (s d)")).then_inc(sl_st, 16)
                sp.wait_ge(sl_st, 16 * T + 16)
                with sp.Fori(0, B) as b:
                    sp.wait_ge(a2_used, b + 1)
                    sp.dma_start(A2.rearrange("p t s d -> p t (s d)"),
                                 at2_dram[ds(b * TB, TB)].rearrange("t p n -> p t n")).then_inc(a2_in, 16)
            sp.wait_ge(h_lo, T)
            with sp.Fori(0, B) as b:
                with sp.If(slow == 1):
                    sp.wait_ge(a2_used, b + B + 1)
                    sp.dma_start(A2.rearrange("p t s d -> p t (s d)"),
                                 at2_dram[ds(b * TB, TB)].rearrange("t p n -> p t n")).then_inc(a2_in, 16)
                for j in range(TB):
                    sp.wait_ge(o_ready, b * TB + j + 1)
                    sp.dma_start(xb[:, j % 2, :], x_p[:, ds(b * TB + j, 1), :].rearrange("p o f -> p (o f)"))\
                        .then_inc(xr_in[j % 2], 16)

        @block.gpsimd
        def _(pool):
            count = [0]

            def link(ins):
                count[0] += 1
                ins.then_inc(pool_chain, 1)
                pool.wait_ge(pool_chain, count[0])

            pool.memset(ident[:, :], 0.0).then_inc(pool_chain, 1)
            pool.memset(ident16[:, :], 0.0).then_inc(pool_chain, 1)
            pool.memset(delta[:, :, :], 1.0).then_inc(pool_chain, 1)
            pool.wait_ge(pool_chain, 3)
            count[0] = 3
            for m in (ident, ident16):
                pool.affine_select(out=m[:, :], in_=m[:, :], compare_op=ALU.not_equal, fill=1.0, base=0,
                                   pattern=[[-1, P]], channel_multiplier=1).then_inc(consts, 1)
            pool.iota(iota16[:, :], pattern=[[1, KEY]], base=0, channel_multiplier=0,
                      allow_small_or_imprecise_dtypes=True).then_inc(consts, 1)
            pool.iota(pidx, pattern=[[0, 1]], base=0, channel_multiplier=1).then_inc(consts, 1)
            pool.iota(wbase, pattern=[[0, 1]], base=0, channel_multiplier=WIN,
                      allow_small_or_imprecise_dtypes=True).then_inc(consts, 1)
            pool.iota(wminus, pattern=[[-1, 8], [1, P]], base=0, channel_multiplier=0,
                      allow_small_or_imprecise_dtypes=True).then_inc(consts, 1)
            link(pool.affine_select(out=delta[:, :, :], in_=delta[:, :, :], compare_op=ALU.is_ge, fill=0.0, base=0,
                                    pattern=[[-16, HB], [0, 8]], channel_multiplier=1))
            pool.affine_select(out=delta[:, :, :], in_=delta[:, :, :], compare_op=ALU.is_ge, fill=0.0, base=15,
                               pattern=[[16, HB], [0, 8]], channel_multiplier=-1).then_inc(consts, 1)
            pool.memset(ones[:, :], 1.0).then_inc(consts, 1)

            def split_low(t):
                pool.wait_ge(h_f32, t + 1)
                pool.tensor_tensor(hs[:, t % 2, 1, :], xb[:, t % 3, :], hs[:, t % 2, 0, :], ALU.subtract)\
                    .then_inc(h_lo, 1)

            for t in range(3):
                split_low(t)
            pool.wait_ge(start_ready, 1)
            for to, of, s in ((srcw, src, src_g), (dstw, dst, dst_g)):
                pool.indirect_dma_start(to, None, of.rearrange("(e o) -> e o", o=1),
                                        bass.IndirectOffsetOnAxis(start.bitcast(u32), 0)).then_inc(s, 16)
            for t in range(3, 9):
                split_low(t)
            pool.wait_ge(wmax_ready, 1)
            pool.partition_all_reduce(wall, wtop, P, bass.bass_isa.ReduceOp.max).then_inc(wall_ready, 1)
            for t in range(9, T):
                split_low(t)
            pool.wait_ge(wmax_ready, 2)
            pool.partition_all_reduce(wall, wtop, P, bass.bass_isa.ReduceOp.max).then_inc(wall_ready, 1)
            pool.wait_ge(hmax_ready, 1)
            pool.partition_all_reduce(hall, htop, P, bass.bass_isa.ReduceOp.max).then_inc(hall_ready, 1)

        @block.scalar
        def _(act):
            def wt_copies(l):
                for k in range(K):
                    act.wait_ge(wt_done, l * K + k + 1)
                    act.activation(raw[l][:, LINT, k, :], ps[WTB[k]][:, :], ACT.Copy).then_inc(wt_copied, 1)

            def layernorm(t):
                act.wait_ge(var_ready, t + 1)
                act.activation(sd, mv[:, 1:2], ACT.Sqrt, bias=epsc, scale=SH ** -2).then_inc(sd_ready, 1)
                act.wait_ge(norm_ready, t + 1)
                if t >= 2:
                    act.wait_ge(tp_done, t - 1)
                act.activation(hs[:, t % 2, 0, :], xb[:, t % 3, :], ACT.Relu, bias=nb[:, t % 2:t % 2 + 1], scale=rs[:, t % 2:t % 2 + 1]).then_inc(h_hi, 1)
                act.activation(xb[:, t % 3, :], xb[:, t % 3, :], ACT.Relu, bias=nb[:, t % 2:t % 2 + 1], scale=rs[:, t % 2:t % 2 + 1]).then_inc(h_f32, 1)

            def fold_copy(l, t):
                act.wait_ge(fold_done, l * 2 * K + t + 1)
                act.activation(Wf[:, l, t, :], ps[FOLD[t % 2]][:, :], ACT.Copy).then_inc(fold_copied, 1)

            def hT_copy(t):
                act.wait_ge(tp_done, t + 1)
                act.activation(H5[:, t + TB], tp16, ACT.Copy).then_inc(hT_ready, 1)

            def w_high(l):
                act.wait_ge(sW_ready, l + 1)
                for c in range(2):
                    act.activation(Wb[:, l, c, 0], Wf[:, l, c * K:(c + 1) * K, :], ACT.Copy, scale=sW[l])\
                        .then_inc(w_hi, 1)

            act.sem_inc(A_ready, 2)
            act.sem_inc(c_lo, K)
            act.sem_inc(o_out[0], 16)
            act.sem_inc(o_out[1], 16)
            act.sem_inc(h1_ready, K)
            act.wait_ge(epsd, 1)
            wt_copies(0)
            for t in range(2 * K):
                layernorm(t)
                fold_copy(0, t)
                hT_copy(t)
            wt_copies(1)
            for t in range(2 * K, T):
                layernorm(t)
                if t == 10:
                    w_high(0)
                fold_copy(1, t - 2 * K)
                hT_copy(t)
            w_high(1)
            act.wait_ge(w_lo, 2)

            with act.Fori(0, T) as i:
                act.wait_ge(y_done, i + 1)
                act.activation(Y4[:, ds(i, 1), 0, :], ps[GY[0]][:, :], ACT.Copy).then_inc(y_hi, 1)
                for q in range(WT // 2):
                    act.wait_ge(win_done, (i + 1) * WT + 2 * q + 2)
                    act.activation(A4[:, ds(i, 1), :, 2 * q * WIN:2 * (q + 1) * WIN].rearrange(
                        "p o s (w d) -> p (o s) w d", w=2),
                        ps[ACC[q % 2]][:, :].rearrange("p (w s d) -> p s w d", w=2, s=HI), ACT.Copy)\
                        .then_inc(A_ready, 1)

            act.wait_ge(flag_set, 1)
            slow = act.value_load(flag[0:1, 0:1], min_val=0, max_val=1)
            with act.If(slow == 1):
                with act.Fori(0, T) as i:
                    with act.Fori(0, WT) as u:
                        act.wait_ge(sl_win, i * WT + u + 1)
                        act.activation(A4[:, ds(i, 1), :, ds(u * WIN, WIN)].rearrange("p o s d -> p (o s) d"),
                                       ps[ACC[0]][:, 0:KEY].rearrange("p (s d) -> p s d", s=HI), ACT.Copy)\
                            .then_inc(sl_A, 1)

            with act.Fori(0, B) as b:
                for k in range(K):
                    act.wait_ge(z1_done, b * K + k + 1)
                    act.activation(H1[:, ds(b, 1), k, :], ps[GZ[k]][:, :], ACT.Relu,
                                   bias=bias1[:, k:k + 1], scale=iS1).then_inc(h1_ready, 1)
            act.wait_ge(sH_ready, 1)
            with act.Fori(0, B) as c:
                act.wait_ge(c_lo, c * K + K)
                act.activation(H5[:, ds(c * -TB + B * TB, TB), 0].rearrange("p t k n -> p k t n"),
                               H1[:, ds(c * -1 + (B - 1), 1)].rearrange("p o k (t n) -> p (o k) t n", t=TB),
                               ACT.Copy, scale=sHs).then_inc(c_hi, 1)
                
            with act.Fori(0, B) as c:
                for j in range(TB):
                    act.wait_ge(y2_done, c * TB + j + 1)
                    act.activation(Y4[:, ds(c * -TB + ((B - 1) * TB + j), 1), 0, :], ps[GY[j % 2]][:, :], ACT.Copy)\
                        .then_inc(y2_hi, 1)
            with act.Fori(0, B) as b:
                for j in range(TB):
                    act.wait_ge(o_ready, b * TB + j + 3)
                    act.dma_start(out_p[:, ds(b * TB + j, 1), :].rearrange("p o f -> p (o f)"), ho[j % 2])\
                        .then_inc(o_out[j % 2], 16)
            for j in range(2):
                act.wait_ge(o_out[j], 16 * (T // 2) + 16)

        @block.vector
        def _(dve):
            count = [0]

            def link(ins):
                count[0] += 1
                ins.then_inc(dve_chain, 1)
                dve.wait_ge(dve_chain, count[0])

            def layernorm(t):
                dve.wait_ge(x_in[t % 3], 16 * (t // 3 + 1))
                link(dve.bn_stats(st6[:, :], xb[:, t % 3, :]))
                dve.bn_aggr(mv, st6[:, :]).then_inc(var_ready, 1)
                dve.wait_ge(sd_ready, t + 1)
                if t >= 2:
                    dve.wait_ge(h_f32, t - 1)
                r, n = rs[:, t % 2:t % 2 + 1], nb[:, t % 2:t % 2 + 1]
                link(dve.reciprocal(r, sd))
                dve.tensor_scalar(n, mv[:, 0:1], r, -1.0, ALU.mult, ALU.mult).then_inc(norm_ready, 1)

            def exponent(v, bits_of_scale, scale, bits_of_inverse, inverse):
                link(dve.tensor_scalar(pint.bitcast(f32), v, 2.0 ** -60, None, ALU.max))
                link(dve.tensor_scalar(ebits, pint, 0x7F800000, None, ALU.bitwise_and))
                link(dve.tensor_scalar(inverse.bitcast(i32), ebits, float(bits_of_inverse << 23), None, ALU.subtract))
                return dve.tensor_scalar(scale.bitcast(i32), ebits, -1.0, float(bits_of_scale << 23), ALU.mult, ALU.add)

            def weight_max(l, t):
                dve.wait_ge(fold_copied, l * 2 * K + t + 1)
                link(dve.tensor_reduce(wmax[:, t:t + 1], Wf[:, l, t, :], X, ALU.max, apply_absolute_value=True))

            def weight_scale(l):
                link(dve.tensor_reduce(wtop, wmax, X, ALU.max))
                dve.sem_inc(wmax_ready, 1)
                dve.wait_ge(wall_ready, l + 1)
                exponent(wall, 255, sW[l], 1, iW[l]).then_inc(sW_ready, 1)
                dve.wait_ge(sW_ready, l + 1)

            def weight_low(l):
                for c in range(2):
                    dve.wait_ge(w_hi, l * 2 + c + 1)
                    ins = dve.scalar_tensor_tensor(Wb[:, l, c, 1], Wf[:, l, c * K:(c + 1) * K, :], sW[l], Wb[:, l, c, 0],
                                                   ALU.mult, ALU.subtract)
                ins.then_inc(w_lo, 1)

            dve.memset(epsc, EPS / SH ** 2).then_inc(epsd, 1)
            dve.sem_inc(onehot_ready, 1)
            dve.sem_inc(sl_oh, 1)
            dve.sem_inc(o_ready, 2)
            dve.wait_ge(dst_in, 16)
            link(dve.tensor_scalar(bit1, dnat, 7, None, ALU.logical_shift_right))
            link(dve.tensor_scalar(bit0, dnat, 4, 7, ALU.logical_shift_right, ALU.bitwise_and))
            dve.wait_ge(consts, 8)
            dve.tensor_tensor(oh1, bit1.unsqueeze(2).to_broadcast([P, EC, 16]),
                              iota16[:, 0:16].unsqueeze(1).to_broadcast([P, EC, 16]), ALU.is_equal)
            dve.tensor_tensor(oh0, bit0.unsqueeze(2).to_broadcast([P, EC, 8]),
                              iota16[:, 0:8].unsqueeze(1).to_broadcast([P, EC, 8]), ALU.is_equal).then_inc(oh_hist, 1)
            link(dve.tensor_scalar(pint, pidx, 15, None, ALU.bitwise_and))
            link(dve.tensor_scalar(b1off, pint, 8.0, None, ALU.mult))
            link(dve.tensor_scalar(before, wminus, b1off, None, ALU.is_gt))
            layernorm(0)
            layernorm(1)
            dve.wait_ge(hist_done, 1)
            link(dve.tensor_tensor(masked, ps[MISC][:, 0:HB * 8].rearrange("p (c b) -> p c b", c=HB), delta[:, :, :], ALU.mult))
            dve.tensor_reduce(hist, masked.rearrange("p c b -> p b c"), X, ALU.add).then_inc(hist_ready, 1)
            layernorm(2)
            layernorm(3)
            dve.wait_ge(start_done, 1)
            dve.tensor_scalar(start, ps[MISC][:, 64:65], float(E - CAP), None, ALU.min).then_inc(start_ready, 1)
            layernorm(4)
            layernorm(5)
            dve.wait_ge(dst_g, 16)
            link(dve.tensor_scalar(rel, dstw, wbase, None, ALU.subtract))
            link(dve.tensor_scalar(bad, rel, 0.0, None, ALU.is_lt))
            link(dve.scalar_tensor_tensor(bad, rel, float(WIN), bad, ALU.is_ge, ALU.add))
            link(dve.tensor_reduce(badsum, bad, X, ALU.add))
            link(dve.scalar_tensor_tensor(key, bad, FAR, rel, ALU.mult, ALU.add))
            dve.wait_ge(src_g, 16)
            link(dve.tensor_scalar(highi, srcw, 3, 0x7F0, ALU.logical_shift_right, ALU.bitwise_and))
            link(dve.tensor_scalar(lowi, srcw, P - 1, None, ALU.bitwise_and))
            link(dve.tensor_tensor(key, key, highi, ALU.add))
            dve.tensor_copy(low, lowi).then_inc(keys_ready, 1)
            dve.wait_ge(keyT_done, 1)
            for v in range(2):
                dve.tensor_copy(keyT[:, v * CH:(v + 1) * CH, :].rearrange("p j w -> p (j w)"),
                                ps[v][:, 0:CH * P]).then_inc(keyT_copied, 1)
            dve.wait_ge(cover_done, 1)
            dve.tensor_scalar(flag, ps[MISC][:, 66:67], float(CAP * P - E), None, ALU.not_equal).then_inc(flag_set, 1)
            for t in range(6, 9):
                layernorm(t)
            for t in range(2 * K):
                weight_max(0, t)
            weight_scale(0)
            layernorm(9)
            layernorm(10)
            weight_low(0)
            for t in range(11, T):
                layernorm(t)
            dve.tensor_scalar(iS1, iW[0], 1 / SH, None, ALU.mult)
            dve.wait_ge(b_in, 48)
            dve.tensor_copy(bcol[:, :, :], brel[:, K:2 * K].unsqueeze(2).to_broadcast([P, K, P])).then_inc(bcol_ready, 1)
            dve.wait_ge(b1_done, 1)
            dve.tensor_tensor(bias1, ps[MISC][:, P:P + K], blin, ALU.add).then_inc(b1_ready, 1)
            for t in range(2 * K):
                weight_max(1, t)
            weight_scale(1)
            weight_low(1)
            dve.wait_ge(b2_done, 1)
            dve.tensor_copy(bias2[:, :], ps[MISC][:, :]).then_inc(b2_ready, 1)

            with dve.Fori(0, T) as i:
                dve.wait_ge(onehot_ready, i * WT + 1)
                dve.tensor_copy(cur[:, :, :], keyT[:, :, ds(i * WT, WT)]).then_inc(cur_ready, 1)
                dve.wait_ge(cur_ready, i + 1)
                for u in range(WT):
                    dve.wait_ge(win_done, i * WT + u + 1)
                    for j in range(CH):
                        dve.tensor_scalar(R4[:, u, j, 0:P], iota16[:, 0:P], cur[:, CH + j, u:u + 1], None, ALU.is_equal)
                        ins = dve.tensor_scalar(R4[:, u, j, P:OH], iota16[:, :], cur[:, j, u:u + 1], None, ALU.is_equal)
                    ins.then_inc(onehot_ready, 1)
                dve.wait_ge(y_hi, i + 1)
                dve.tensor_tensor(Y4[:, ds(i, 1), 1, :].rearrange("p o f -> p (o f)"), ps[GY[0]][:, :],
                                  Y4[:, ds(i, 1), 0, :].rearrange("p o f -> p (o f)"), ALU.subtract).then_inc(y_lo, 1)

            slow = dve.value_load(flag[0:1, 0:1], min_val=0, max_val=1)
            with dve.If(slow == 1):
                dve.wait_ge(sl_in, 32)
                dve.tensor_scalar(s_lowi, s_src, P - 1, None, ALU.bitwise_and).then_inc(sl_chain, 1)
                dve.wait_ge(sl_chain, 1)
                dve.tensor_copy(s_low, s_lowi).then_inc(sl_chain, 1)
                dve.tensor_scalar(s_high, s_src, 3, 0x7F0, ALU.logical_shift_right, ALU.bitwise_and).then_inc(sl_chain, 1)
                dve.tensor_copy(s_rel, s_dst).then_inc(sl_chain, 1)
                dve.wait_ge(sl_chain, 4)
                with dve.Fori(0, T) as i:
                    with dve.Fori(0, WT) as u:
                        w = i * WT + u
                        c = 4 + w * 5
                        dve.tensor_scalar(s_tmp, s_rel, 0.0, None, ALU.is_lt).then_inc(sl_chain, 1)
                        dve.wait_ge(sl_chain, c + 1)
                        dve.scalar_tensor_tensor(s_tmp, s_rel, float(WIN), s_tmp, ALU.is_ge, ALU.add).then_inc(sl_chain, 1)
                        dve.wait_ge(sl_chain, c + 2)
                        dve.wait_ge(sl_oh, w * EC + 1)
                        dve.scalar_tensor_tensor(s_key, s_tmp, FAR, s_rel, ALU.mult, ALU.add).then_inc(sl_chain, 1)
                        dve.wait_ge(sl_chain, c + 3)
                        dve.tensor_tensor(s_key, s_key, s_high, ALU.add).then_inc(sl_chain, 1)
                        dve.tensor_scalar(s_rel, s_rel, -float(WIN), None, ALU.add).then_inc(sl_chain, 1)
                        with dve.Fori(0, EC // 2) as m:
                            for h in range(2):
                                dve.wait_ge(sl_chain, c + 5)
                                dve.wait_ge(sl_free, w * EC + 2 * m + h + 1)
                                dve.tensor_scalar(s_oh[h][:, 0:P], iota16[:, 0:P], s_low[:, ds(2 * m + h, 1)], None,
                                                  ALU.is_equal)
                                dve.tensor_scalar(s_oh[h][:, P:OH], iota16[:, :], s_key[:, ds(2 * m + h, 1)], None,
                                                  ALU.is_equal).then_inc(sl_oh, 1)
                        dve.wait_ge(sl_A, w + 1)
                        dve.wait_ge(sl_st, 16 * i + 16)
                        dve.tensor_tensor(A2s[:, :, ds(u * WIN, WIN)],
                                          ps[ACC[0]][:, 0:KEY].rearrange("p (s d) -> p s d", s=HI),
                                          A4[:, ds(i, 1), :, ds(u * WIN, WIN)].rearrange("p o s d -> p (o s) d"),
                                          ALU.subtract).then_inc(sl_A2, 1)

            with dve.Fori(0, B) as b:
                for k in range(K):
                    dve.wait_ge(h1_ready, b * K + k + 1 + K)
                    dve.tensor_reduce(hmax[:, ds(b * K + k, 1)], H1[:, ds(b, 1), k, :].rearrange("p o n -> p (o n)"),
                                      X, ALU.max).then_inc(hmax_part, 1)
            dve.wait_ge(hmax_part, B * K)
            link(dve.tensor_reduce(htop, hmax, X, ALU.max))
            dve.sem_inc(hmax_ready, 1)
            dve.wait_ge(hall_ready, 1)
            exponent(hall, 257, sHs, 3, iH).then_inc(sH_ready, 1)
            dve.wait_ge(sH_ready, 1)
            link(dve.tensor_tensor(iS2, iH, iW[1], ALU.mult))
            with dve.Fori(0, B) as c:
                dve.wait_ge(c_hi, c + 1)
                for k in range(K):
                    dve.scalar_tensor_tensor(
                        H5[:, ds(c * -TB + B * TB, TB), 1, k, :],
                        H1[:, ds(c * -1 + (B - 1), 1), k].rearrange("p o (t n) -> p (o t) n", t=TB), sHs,
                        H5[:, ds(c * -TB + B * TB, TB), 0, k, :], ALU.mult, ALU.subtract).then_inc(c_lo, 1)
            with dve.Fori(0, B) as c:
                for j in range(TB):
                    dve.wait_ge(y2_hi, c * TB + j + 1)
                    n = c * -TB + ((B - 1) * TB + j)
                    dve.tensor_tensor(Y4[:, ds(n, 1), 1, :].rearrange("p o f -> p (o f)"), ps[GY[j % 2]][:, :],
                                      Y4[:, ds(n, 1), 0, :].rearrange("p o f -> p (o f)"), ALU.subtract).then_inc(y2_lo, 1)
            with dve.Fori(0, B) as b:
                for j in range(TB):
                    dve.wait_ge(z2_done, b * TB + j + 1)
                    dve.wait_ge(o_out[j % 2], (b * (TB // 2) + j // 2 + 1) * 16)
                    dve.scalar_tensor_tensor(ho[j % 2], ps[GZ[j]][:, :], iS2, bias2[:, :], ALU.mult, ALU.add)\
                        .then_inc(z2_read, 1)
                    dve.wait_ge(z2_read, b * TB + j + 1 + TB)
                    dve.wait_ge(xr_in[j % 2], (b * (TB // 2) + j // 2 + 1) * 16)
                    dve.scalar_tensor_tensor(ho[j % 2], ho[j % 2], 0.0, xb[:, j % 2, :], ALU.max, ALU.add)\
                        .then_inc(o_ready, 1)

        @block.tensor
        def _(pe):
            def transpose_lin(l):
                pe.wait_ge(w_in[l][LIN], 16)
                if l == 1:
                    pe.wait_ge(keyT_copied, 2)
                for k in range(K):
                    for q in range(K):
                        ins = pe.transpose(ps[WTB[k]][:, q * P:(q + 1) * P], raw[l][:, LIN, q, k * P:(k + 1) * P], ident[:, :])
                    ins.then_inc(wt_done, 1)

            def fold(l, t):
                c, q = t // K, t % K
                if t % K == 0:
                    pe.wait_ge(w_in[l][c], 16)
                if t == 0:
                    pe.wait_ge(wt_copied, (l + 1) * K)
                g = l * 2 * K + t
                if g >= 2:
                    pe.wait_ge(fold_copied, g - 1)
                for k in range(K):
                    ins = pe.matmul(ps[FOLD[t % 2]][:, :], raw[l][:, c, k, q * P:(q + 1) * P], raw[l][:, LINT, k, :],
                                    start=(k == 0), stop=(k == K - 1))
                ins.then_inc(fold_done, 1)

            def transpose_h(t):
                pe.wait_ge(h_lo, t + 1)
                if t >= 1:
                    pe.wait_ge(hT_ready, t)
                for a in range(2):
                    for k in range(K):
                        ins = pe.transpose(tp16[:, a, k, :], hs[:, t % 2, a, k * P:(k + 1) * P], ident16[:, :])
                ins.then_inc(tp_done, 1)

            def split_products(out_, left, right):
                terms = [(k, a, b) for k in range(K) for a, b in ((0, 0), (0, 1), (1, 0))]
                return [(out_, left(k, a), right(k, b)) for k, a, b in terms]

            pe.sem_inc(win_done, WT)
            pe.sem_inc(y_lo, 1)
            pe.wait_ge(consts, 8)
            transpose_lin(0)
            for t in range(2 * K):
                fold(0, t)
                if t == 1:
                    pe.wait_ge(oh_hist, 1)
                    for c in range(0, EC, HB):
                        ins = pe.matmul(ps[MISC][:, 0:HB * 8], oh1[:, c:c + HB, :].rearrange("p c v -> p (c v)"),
                                        oh0[:, c:c + HB, :].rearrange("p c v -> p (c v)"),
                                        start=(c == 0), stop=(c == EC - HB))
                    ins.then_inc(hist_done, 1)
                if t == 3:
                    pe.wait_ge(hist_ready, 1)
                    for b in range(8):
                        ins = pe.matmul(ps[MISC][:, 64:65], before[:, b, :], hist[:, b:b + 1], start=(b == 0), stop=(b == 7))
                    ins.then_inc(start_done, 1)
                transpose_h(t)
                if t == 5:
                    pe.wait_ge(keys_ready, 1)
                    for v, rows in enumerate((key, low)):
                        for j in range(CH):
                            ins = pe.transpose(ps[v][:, j * P:(j + 1) * P], rows[:, j * P:(j + 1) * P], ident[:, :])
                    ins.then_inc(keyT_done, 1)
                    pe.matmul(ps[MISC][:, 66:67], ones[:, :], badsum, start=True, stop=True).then_inc(cover_done, 1)
            pe.wait_ge(b_in, 48)
            for q in range(K):
                for k in range(K):
                    ins = pe.matmul(ps[MISC][:, P + q:P + q + 1], raw[0][:, LINT, k, q * P:(q + 1) * P], brel[:, k:k + 1],
                                    start=(k == 0), stop=(k == K - 1))
            ins.then_inc(b1_done, 1)
            transpose_lin(1)
            for t in range(2 * K):
                fold(1, t)
                transpose_h(2 * K + t)
            pe.wait_ge(bcol_ready, 1)
            pe.wait_ge(b1_ready, 1)
            pe.wait_ge(brow_in, 16)
            for k in range(K):
                pe.matmul(ps[MISC][:, :], bcol[:, k, :], raw[1][:, LINT, k, :], start=(k == 0), stop=False)
            pe.matmul(ps[MISC][:, :], ones[0:1, :], brow[0:1, :], start=False, stop=True).then_inc(b2_done, 1)

            pe.wait_ge(w_lo, 1)
            pe.wait_ge(hT_ready, T)
            with pe.Fori(0, T) as i:
                pe.wait_ge(y_lo, i + 1)
                todo = split_products(ps[GY[0]][:, :], lambda k, a: H5[:, ds(i + TB, 1), a, k, :].rearrange("p o n -> p (o n)"),
                                      lambda k, b: Wb[:, 0, 0, b, k, :])
                for n, (o_, l_, r_) in enumerate(todo):
                    ins = pe.matmul(o_, l_, r_, start=(n == 0), stop=(n == len(todo) - 1))
                ins.then_inc(y_done, 1)
                for u in range(WT):
                    if u % 2 == 0:
                        pe.wait_ge(A_ready, i * (WT // 2) + u // 2 + 1)
                    pe.wait_ge(onehot_ready, i * WT + u + 2)
                    for j in range(CH):
                        ins = pe.matmul(ps[ACC[u // 2 % 2]][:, u % 2 * KEY:(u % 2 + 1) * KEY], R4[:, u, j, 0:P], R4[:, u, j, P:OH],
                                        start=(j == 0), stop=(j == CH - 1))
                    ins.then_inc(win_done, 1)

            pe.wait_ge(A_ready, T * WT // 2 + 2)
            pe.wait_ge(flag_set, 1)
            slow = pe.value_load(flag[0:1, 0:1], min_val=0, max_val=1)
            with pe.If(slow == 1):
                pe.sem_inc(sl_free, 2)
                pe.sem_inc(a2_used, 1)
                pe.sem_inc(sl_A2, 1)
                with pe.Fori(0, T * WT) as w:
                    pe.wait_ge(sl_A2, w + 1)

                    def pair(chunk, first, last):
                        for h in range(2):
                            pe.wait_ge(sl_oh, chunk + h + 2)
                            ins = pe.matmul(ps[ACC[0]][:, 0:KEY], s_oh[h][:, 0:P], s_oh[h][:, P:OH],
                                            start=first and h == 0, stop=last and h == 1)
                            ins.then_inc(sl_free, 1)

                    pair(w * EC, True, False)
                    with pe.Fori(1, EC // 2 - 1) as m:
                        pair(w * EC + 2 * m, False, False)
                    pair(w * EC + EC - 2, False, True)
                    pe.wait_ge(sl_free, w * EC + EC + 2)
                    pe.sem_inc(sl_win, 1)
                pe.wait_ge(sl_A2, T * WT + 1)

            pe.wait_ge(y_lo, T + 1)
            with pe.Fori(0, B) as b:
                for q in range(K):
                    z = ps[GZ[q]][:, :].rearrange("p (t n) -> p t n", t=TB)
                    cols = slice(q * P, (q + 1) * P)
                    pe.wait_ge(h1_ready, b * K + q + 1)
                    todo = split_products(z, lambda k, a: Wb[:, 0, 1, a, k, cols], lambda k, c: H5[:, ds(b * TB + TB, TB), c, k, :])
                    for n, (o_, l_, r_) in enumerate(todo):
                        pe.matmul(o_, l_, r_, start=(n == 0), stop=False)
                    if True:
                        with pe.If(slow == 1):
                            pe.wait_ge(a2_in, 16 * b + 16)
                            for s in range(HI):
                                for a in range(2):
                                    pe.matmul(z, Y4[:, s, a, cols], A2[:, :, s, :], start=False, stop=False)
                    for s in range(HI):
                        for a in range(2):
                            ins = pe.matmul(z, Y4[:, s, a, cols], A4[:, ds(b * TB, TB), s, :],
                                            start=False, stop=(s == HI - 1 and a == 1))
                    ins.then_inc(z1_done, 1)
                with pe.If(slow == 1):
                    pe.drain().then_inc(a2_used, 1)

            pe.sem_inc(y2_lo, 2)
            pe.sem_inc(z2_read, TB)
            with pe.Fori(0, B) as c:
                pe.wait_ge(c_lo, c * K + 2 * K)
                for j in range(TB):
                    pe.wait_ge(y2_lo, c * TB + j + 1)
                    todo = split_products(ps[GY[j % 2]][:, :],
                                          lambda k, a: H5[:, ds(c * -TB + (B * TB + j), 1), a, k, :].rearrange("p o n -> p (o n)"),
                                          lambda k, b: Wb[:, 1, 0, b, k, :])
                    for n, (o_, l_, r_) in enumerate(todo):
                        ins = pe.matmul(o_, l_, r_, start=(n == 0), stop=(n == len(todo) - 1))
                    ins.then_inc(y2_done, 1)

            with pe.Fori(0, B) as b:
                for j in range(TB):
                    z = ps[GZ[j]][:, :]
                    pe.wait_ge(z2_read, b * TB + j + 1)
                    todo = split_products(z, lambda k, a: H5[:, ds((b + 1) * TB + j, 1), a, k, :].rearrange("p o n -> p (o n)"),
                                          lambda k, c: Wb[:, 1, 1, c, k, :])
                    for n, (o_, l_, r_) in enumerate(todo):
                        pe.matmul(o_, l_, r_, start=(n == 0), stop=False)
                    pe.wait_ge(y2_lo, T + 2)
                    with pe.If(slow == 1):
                        pe.wait_ge(a2_in, 16 * b + 16 * B + 16)
                        for s in range(HI):
                            for a in range(2):
                                pe.matmul(z, A2[:, j, s, :], Y4[:, s, a, :], start=False, stop=False)
                    for s in range(HI):
                        for a in range(2):
                            ins = pe.matmul(z, A4[:, ds(b * TB + j, 1), s, :].rearrange("p o n -> p (o n)"), Y4[:, s, a, :],
                                            start=False, stop=(s == HI - 1 and a == 1))
                    ins.then_inc(z2_done, 1)
                with pe.If(slow == 1):
                    pe.drain().then_inc(a2_used, 1)


_INS = ["x", "src", "dst"] + [f"L0_gnn_{n}" for n in ("W_rel1", "b_rel1", "W_root1", "W_lin1", "b_lin1",
                                                     "W_rel2", "b_rel2", "W_root2", "W_lin2", "b_lin2")]


def kernel(**inputs):
    import numpy as _np
    import concourse.bacc as _bacc
    from concourse import mybir as _mybir
    from concourse.bass_utils import run_bass_kernel_spmd as _run

    nc = _bacc.Bacc("TRN2", target_bir_lowering=False, num_devices=1)
    arrays, args = {}, []
    for name in _INS:
        a = _np.ascontiguousarray(inputs[name])
        arrays[f"in_{name}"] = a
        args.append(nc.dram_tensor(f"in_{name}", a.shape, _mybir.dt.from_np(a.dtype), kind="ExternalInput").ap())
    out = nc.dram_tensor("out_0", inputs["x"].shape, _mybir.dt.float32, kind="ExternalOutput").ap()
    gnn_block_kernel(nc, *args, out)
    return _run(nc, [arrays], core_ids=[0]).results[0]["out_0"]
```

```python
import numpy as np
import concourse.bass as bass
from concourse import mybir
from contextlib import ExitStack


def gnn_block_kernel(nc, x, src, dst, W_rel1, b_rel1, W_root1, W_lin1, b_lin1,
                     W_rel2, b_rel2, W_root2, W_lin2, b_lin2, out):
    f32, f16 = mybir.dt.float32, mybir.dt.float16
    i32, u32 = mybir.dt.int32, mybir.dt.uint32
    ALU = mybir.AluOpType
    ACT = mybir.ActivationFunctionType
    X = mybir.AxisListType.X
    ds = bass.ds

    P = 128
    N, F = x.shape
    E = src.shape[0]
    T = N // P
    K = F // P
    B = 4
    TB = T // B
    NB = N // B
    WIN = N // P
    WT = P // WIN
    HI = N // P
    KEY = HI * WIN
    CH = 3
    CAP = CH * P
    EC = E // P
    OH = P + KEY
    ST = WT * CH
    SIDE = 4
    HG = ST // 2 // SIDE
    HB = 8
    FAR = 4096.0
    EPS = 1e-5
    SH = 16.0
    REL, ROOT, LIN, LINT = range(4)
    assert N == WIN * P and HI * WIN == KEY and E == EC * P and KEY == 256 and EC % HB == 0

    at2_dram = nc.dram_tensor("at2", (T, P, HI * P), f16, kind="Internal").ap()
    x_t = x.rearrange("(t p) f -> t p f", p=P)
    x_p = x.rearrange("(t p) f -> p t f", p=P)
    out_p = out.rearrange("(t p) f -> p t f", p=P)

    ctx = ExitStack()
    with ctx:
        def sb(name, shape, dt):
            return ctx.enter_context(nc.sbuf_tensor(name, shape, dt))

        def sem(name):
            return ctx.enter_context(nc.semaphore(name))

        At = sb("At", [P, T * HI * P], f16)
        A4 = At[:, :].rearrange("p (t s d) -> p t s d", t=T, s=HI)
        Yt = sb("Yt", [P, T * 2 * F], f16)
        Y4 = Yt[:, :].rearrange("p (t a f) -> p t a f", t=T, a=2)
        Ht = sb("Ht", [P, (B + 1) * TB * 2 * K * P], f16)
        H5 = Ht[:, :].rearrange("p (t a k n) -> p t a k n", a=2, k=K, n=P)
        Hf = Ht[:, :].bitcast(f32)
        H1 = Hf.rearrange("p (b k n) -> p b k n", b=B + 1, k=K)
        Wb = sb("Wb", [P, 2, 2, 2, K, F], f16)
        ring = sb("ring", [P, ST * OH], f16)
        R4 = ring[:, :].rearrange("p (g c r) -> p g c r", c=OH, r=SIDE)
        xb = sb("xb", [P, 3, F], f32)
        hs = sb("hs", [P, 2, 2, F], f16)
        bias2 = sb("bias2", [P, F], f32)
        ident = sb("ident", [P, P], f32)
        ident16 = sb("ident16", [P, P], f16)
        ones = sb("ones", [P, P], f32)
        iota4 = sb("iota4", [P, KEY, SIDE], f16)
        iota16 = iota4[:, :, 0]
        keyT = sb("keyT", [P, 2, P * CH], f16)
        delta = sb("delta", [P, HB, 8], f32)
        small = sb("small", [P, 96], f32)
        smi = sb("smi", [P, 16], i32)
        st6 = sb("st6", [P, 6], f32)
        brow = sb("brow", [1, F], f32)
        bcol = sb("bcol", [P, K, P], f32)

        raw = [Yt[:, :].bitcast(f32).rearrange("p (w k f) -> p w k f", w=4, k=K),
               At[:, T * HI * P // 2:].bitcast(f32).rearrange("p (w k f) -> p w k f", w=4, k=K)]
        Wf = At[:, 0:4 * 2 * K * F].bitcast(f32).rearrange("p (l t f) -> p l t f", l=2, t=2 * K)

        def part(base, at, n, dt):
            v = base[:, at:at + n]
            return v if dt == f32 else v.bitcast(dt)

        srcw, dstw, rel, bad, key = [part(Hf, i * CAP, CAP, dt) for i, dt in enumerate((i32, i32, f32, f32, f32))]
        SL = TB * K * P
        oh1 = Hf[:, 3 * SL:3 * SL + EC * 8].bitcast(f16).rearrange("p (c v) -> p c v", v=16)
        oh0 = Hf[:, 3 * SL + EC * 8:3 * SL + EC * 12].bitcast(f16).rearrange("p (c v) -> p c v", v=8)
        rf = ring[:, :].bitcast(f32)
        before = rf[:, 0:8 * P].rearrange("p (b w) -> p b w", b=8)
        wminus = rf[:, 8 * P:16 * P].rearrange("p (b w) -> p b w", b=8)
        dnat, bit1, bit0 = [part(rf, 16 * P + i * EC, EC, i32) for i in range(3)]
        o = 16 * P + 3 * EC
        lowi, highi, low = part(rf, o, CAP, i32), part(rf, o + CAP, CAP, i32), part(rf, o + 2 * CAP, CAP, f32)
        masked = key[:, 0:HB * 8].rearrange("p (c b) -> p c b", c=HB)

        s_src, s_dst, s_low, s_high, s_rel, s_key, s_tmp = [
            part(Hf, i * EC, EC, dt) for i, dt in enumerate((i32, i32, f32, i32, f32, f32, f32))]
        s_lowi = s_tmp.bitcast(i32)
        s_oh = [ring[:, i * OH:(i + 1) * OH] for i in range(2)]
        A2s = ring[:, 2 * OH:2 * OH + HI * P].rearrange("p (s d) -> p s d", s=HI)
        A2 = ring[:, 0:TB * HI * P].rearrange("p (t s d) -> p t s d", t=TB, s=HI)

        ho = [hs[:, j].rearrange("p a f -> p (a f)").bitcast(f32) for j in range(2)]

        at = [0]

        def col(n):
            at[0] += n
            return small[:, at[0] - n:at[0]]

        hist, wbase, b1off = col(8), col(1), col(1)
        badsum, mv, sd, rs, nb, uvar, rinv = col(1), col(2), col(1), col(2), col(2), col(1), col(1)
        wmax, wtop, wall, brel, blin, bias1 = col(2 * K), col(1), col(1), col(2 * K), col(K), col(K)
        sW = [col(1), col(1)]
        iW = [col(1), col(1)]
        hmax, htop, hall, sHs, iH, iS1, iS2 = col(B * K), col(1), col(1), col(1), col(1), col(1), col(1)
        start, pint, flag, ebits, pidx = smi[:, 0:1], smi[:, 1:2], smi[:, 2:3], smi[:, 3:4], smi[:, 4:5]

        ps = [ctx.enter_context(nc.psum_tensor(f"ps{i}", [P, F], f32)) for i in range(8)]
        ACC = (0, 1)
        TP = 2
        GY = (3, 4)
        FOLD = (5, 6)
        MISC = 7
        GZ = (5, 6, 0, 1)
        WTB = (3, 4, 0, 1)
        tp16 = ps[TP][:, :].bitcast(f16).rearrange("p (a k n) -> p a k n", a=2, k=K)

        dst_in, brow_in, b_in = sem("dst_in"), sem("brow_in"), sem("b_in")
        w_in = [[sem(f"w_in{l}{w}") for w in range(3)] for l in range(2)]
        lin_in = [sem(f"lin_in{q}") for q in range(K)]
        x_in = [sem(f"x_in{i}") for i in range(3)]
        src_g, dst_g = sem("src_gathered"), sem("dst_gathered")
        consts = sem("consts")
        pool_chain, dve_chain = sem("pool_chain"), sem("dve_chain")
        wt_done, wt_copied = sem("wt_done"), sem("wt_copied")
        fold_done, fold_copied = sem("fold_done"), sem("fold_copied")
        oh_hist, hist_done, hist_ready, start_done, start_ready = [
            sem(n) for n in ("hist_onehots", "hist_done", "hist_ready", "start_done", "start_ready")]
        keys_ready, keyT_done, cover_done, flag_set = [sem(n) for n in ("keys_ready", "keyT_done", "cover_done", "flag_set")]
        hmax_part = sem("hmax_part")
        keyT_copied = sem("keyT_copied")
        var_ready, sd_ready, norm_ready = sem("var_ready"), sem("sd_ready"), sem("norm_ready")
        h_hi, h_f32, h_lo = sem("h_hi"), sem("h_f32"), sem("h_lo")
        tp_done, hT_ready = sem("tp_done"), sem("hT_ready")
        wmax_ready, wall_ready, sW_ready, w_hi, w_lo = [sem(n) for n in ("wmax_ready", "wall_ready", "sW_ready", "w_hi", "w_lo")]
        b1_done, b1_ready, bcol_ready, b2_done, b2_ready = [sem(n) for n in ("b1_done", "b1_ready", "bcol_ready", "b2_done", "b2_ready")]
        onehot_ready, pair_done = sem("onehot_ready"), sem("pair_done")
        A_ready = sem("A_ready")
        y_done, y_f32, y_lo = sem("y_done"), sem("y_f32"), sem("y_lo")
        z1_done, h1_ready, hmax_ready, hall_ready, sH_ready = [
            sem(n) for n in ("z1_done", "h1_ready", "hmax_ready", "hall_ready", "sH_ready")]
        c_hi, c_lo = sem("c_hi"), sem("c_lo")
        y2_done, y2_hi, y2_lo = sem("y2_done"), sem("y2_hi"), sem("y2_lo")
        z2_done, z2_read, o_ready = sem("z2_done"), sem("z2_read"), sem("o_ready")
        xr_in = [sem(f"xr_in{i}") for i in range(2)]
        o_out = [sem(f"o_out{i}") for i in range(2)]
        sl_in, sl_oh, sl_free, sl_win, sl_A, sl_A2, sl_st, sl_chain = [
            sem(n) for n in ("slow_in", "slow_onehot", "slow_free", "slow_window", "slow_A", "slow_A2", "slow_stored", "slow_chain")]
        a2_in, a2_used = sem("a2_in"), sem("a2_used")

        block = ctx.enter_context(nc.Block())

        @block.sync
        def _(sp):
            W = ((W_rel1, W_root1, W_lin1), (W_rel2, W_root2, W_lin2))

            def load_w(l, w):
                sp.dma_start(raw[l][:, w], W[l][w].rearrange("(k p) f -> p k f", p=P)).then_inc(w_in[l][w], 16)

            def load_x(t):
                if t >= 3:
                    sp.wait_ge(h_lo, t - 2)
                sp.dma_start(xb[:, t % 3, :], x_t[t]).then_inc(x_in[t % 3], 16)

            sp.dma_start(dnat, dst.rearrange("(p c) -> p c", p=P)).then_inc(dst_in, 16)
            for q in range(K):
                sp.dma_start(raw[0][:, LIN, q], W_lin1[q * P:(q + 1) * P, :]).then_inc(lin_in[q], 16)
            load_w(0, REL)
            load_x(0)
            load_x(1)
            load_x(2)
            load_w(0, ROOT)
            sp.dma_start(brow[:, :], b_lin2.rearrange("(a f) -> a f", a=1)).then_inc(brow_in, 16)
            for v, d in ((brel[:, 0:K], b_rel1), (brel[:, K:2 * K], b_rel2), (blin, b_lin1)):
                sp.dma_start(v, d.rearrange("(k p) -> p k", p=P), allow_slow_non_contiguous=True).then_inc(b_in, 16)
            load_x(3)
            load_w(1, LIN)
            load_w(1, REL)
            load_w(1, ROOT)
            for t in range(4, T):
                load_x(t)

            sp.sem_inc(sl_st, 16)
            sp.wait_ge(flag_set, 1)
            slow = sp.value_load(flag[0:1, 0:1], min_val=0, max_val=1)
            with sp.If(slow == 1):
                sp.wait_ge(A_ready, T * WT // 2 + 2)
                sp.dma_start(s_src, src.rearrange("(p c) -> p c", p=P)).then_inc(sl_in, 16)
                sp.dma_start(s_dst, dst.rearrange("(p c) -> p c", p=P)).then_inc(sl_in, 16)
                with sp.Fori(0, T) as i:
                    sp.wait_ge(sl_A2, (i + 1) * WT + 1)
                    sp.dma_start(at2_dram[ds(i, 1)].rearrange("o p n -> (o p) n"),
                                 A2s.rearrange("p s d -> p (s d)")).then_inc(sl_st, 16)
                sp.wait_ge(sl_st, 16 * T + 16)
                with sp.Fori(0, B) as b:
                    sp.wait_ge(a2_used, b + 1)
                    sp.dma_start(A2.rearrange("p t s d -> p t (s d)"),
                                 at2_dram[ds(b * TB, TB)].rearrange("t p n -> p t n")).then_inc(a2_in, 16)
            sp.wait_ge(h_lo, T)
            with sp.Fori(0, B) as b:
                with sp.If(slow == 1):
                    sp.wait_ge(a2_used, b + B + 1)
                    sp.dma_start(A2.rearrange("p t s d -> p t (s d)"),
                                 at2_dram[ds(b * TB, TB)].rearrange("t p n -> p t n")).then_inc(a2_in, 16)
                for j in range(TB):
                    sp.wait_ge(o_ready, b * TB + j + 1)
                    sp.dma_start(xb[:, j % 2, :], x_p[:, ds(b * TB + j, 1), :].rearrange("p o f -> p (o f)"))\
                        .then_inc(xr_in[j % 2], 16)

        @block.gpsimd
        def _(pool):
            count = [0]

            def link(ins):
                count[0] += 1
                ins.then_inc(pool_chain, 1)
                pool.wait_ge(pool_chain, count[0])

            pool.memset(ident[:, :], 0.0).then_inc(pool_chain, 1)
            pool.memset(ident16[:, :], 0.0).then_inc(pool_chain, 1)
            pool.memset(delta[:, :, :], 1.0).then_inc(pool_chain, 1)
            pool.wait_ge(pool_chain, 3)
            count[0] = 3
            for m in (ident, ident16):
                pool.affine_select(out=m[:, :], in_=m[:, :], compare_op=ALU.not_equal, fill=1.0, base=0,
                                   pattern=[[-1, P]], channel_multiplier=1).then_inc(consts, 1)
            pool.iota(iota4[:, :, :], pattern=[[1, KEY], [0, SIDE]], base=0, channel_multiplier=0,
                      allow_small_or_imprecise_dtypes=True).then_inc(consts, 1)
            pool.iota(pidx, pattern=[[0, 1]], base=0, channel_multiplier=1).then_inc(consts, 1)
            pool.iota(wbase, pattern=[[0, 1]], base=0, channel_multiplier=WIN,
                      allow_small_or_imprecise_dtypes=True).then_inc(consts, 1)
            pool.iota(wminus, pattern=[[-1, 8], [1, P]], base=0, channel_multiplier=0,
                      allow_small_or_imprecise_dtypes=True).then_inc(consts, 1)
            link(pool.affine_select(out=delta[:, :, :], in_=delta[:, :, :], compare_op=ALU.is_ge, fill=0.0, base=0,
                                    pattern=[[-16, HB], [0, 8]], channel_multiplier=1))
            pool.affine_select(out=delta[:, :, :], in_=delta[:, :, :], compare_op=ALU.is_ge, fill=0.0, base=15,
                               pattern=[[16, HB], [0, 8]], channel_multiplier=-1).then_inc(consts, 1)
            pool.memset(ones[:, :], 1.0).then_inc(consts, 1)

            def split_low(t):
                pool.wait_ge(h_f32, t + 1)
                pool.tensor_tensor(hs[:, t % 2, 1, :], xb[:, t % 3, :], hs[:, t % 2, 0, :], ALU.subtract)\
                    .then_inc(h_lo, 1)

            for t in range(3):
                split_low(t)
            pool.wait_ge(start_ready, 1)
            for to, of, s in ((srcw, src, src_g), (dstw, dst, dst_g)):
                pool.indirect_dma_start(to, None, of.rearrange("(e o) -> e o", o=1),
                                        bass.IndirectOffsetOnAxis(start.bitcast(u32), 0)).then_inc(s, 16)
            for t in range(3, 9):
                split_low(t)
            pool.wait_ge(wmax_ready, 1)
            pool.partition_all_reduce(wall, wtop, P, bass.bass_isa.ReduceOp.max).then_inc(wall_ready, 1)
            for t in range(9, T):
                split_low(t)
            pool.wait_ge(wmax_ready, 2)
            pool.partition_all_reduce(wall, wtop, P, bass.bass_isa.ReduceOp.max).then_inc(wall_ready, 1)
            with pool.Fori(0, T) as i:
                pool.wait_ge(y_f32, i + 2)
                pool.tensor_tensor(Y4[:, ds(i, 1), 1, :].rearrange("p o f -> p (o f)"), xb[:, 2, :],
                                   Y4[:, ds(i, 1), 0, :].rearrange("p o f -> p (o f)"), ALU.subtract).then_inc(y_lo, 1)
            pool.wait_ge(hmax_ready, 1)
            pool.partition_all_reduce(hall, htop, P, bass.bass_isa.ReduceOp.max).then_inc(hall_ready, 1)

        @block.scalar
        def _(act):
            def wt_copies(l):
                for k in range(K):
                    act.wait_ge(wt_done, l * K + k + 1)
                    act.activation(raw[l][:, LINT, k, :], ps[WTB[k]][:, :], ACT.Copy).then_inc(wt_copied, 1)

            def layernorm(t):
                act.wait_ge(var_ready, t + 1)
                act.activation(sd, uvar, ACT.Sqrt).then_inc(sd_ready, 1)
                act.wait_ge(norm_ready, t + 1)
                if t >= 2:
                    act.wait_ge(tp_done, t - 1)
                act.activation(hs[:, t % 2, 0, :], xb[:, t % 3, :], ACT.Relu, bias=nb[:, t % 2:t % 2 + 1], scale=rs[:, t % 2:t % 2 + 1]).then_inc(h_hi, 1)
                act.activation(xb[:, t % 3, :], xb[:, t % 3, :], ACT.Relu, bias=nb[:, t % 2:t % 2 + 1], scale=rs[:, t % 2:t % 2 + 1]).then_inc(h_f32, 1)

            def fold_copy(l, t):
                act.wait_ge(fold_done, l * 2 * K + t + 1)
                act.activation(Wf[:, l, t, :], ps[FOLD[t % 2]][:, :], ACT.Copy).then_inc(fold_copied, 1)

            def hT_copy(t):
                act.wait_ge(tp_done, t + 1)
                act.activation(H5[:, t + TB], tp16, ACT.Copy).then_inc(hT_ready, 1)

            def w_high(l):
                act.wait_ge(sW_ready, l + 1)
                for c in range(2):
                    act.activation(Wb[:, l, c, 0], Wf[:, l, c * K:(c + 1) * K, :], ACT.Copy, scale=sW[l])\
                        .then_inc(w_hi, 1)

            act.sem_inc(A_ready, 2)
            act.sem_inc(c_lo, TB)
            act.sem_inc(o_out[0], 16)
            act.sem_inc(o_out[1], 16)
            act.sem_inc(h1_ready, K)
            wt_copies(0)
            layernorm(0)
            for t in range(T):
                if t == 2 * K:
                    wt_copies(1)
                if t + 1 < T:
                    layernorm(t + 1)
                if t == 9:
                    w_high(0)
                fold_copy(t // (2 * K), t % (2 * K))
                hT_copy(t)
            w_high(1)

            with act.Fori(0, T) as i:
                act.wait_ge(y_done, i + 1)
                act.activation(Y4[:, ds(i, 1), 0, :], ps[GY[0]][:, :], ACT.Copy)
                act.wait_ge(y_lo, i + 1)
                act.activation(xb[:, 2, :], ps[GY[0]][:, :], ACT.Copy).then_inc(y_f32, 1)
                act.wait_ge(w_lo, 2)
                for q in range(WT // 2):
                    act.wait_ge(pair_done, i * (WT // 2) + q + 1 + WT // 2)
                    act.activation(A4[:, ds(i, 1), :, 2 * q * WIN:2 * (q + 1) * WIN].rearrange(
                        "p o s (w d) -> p (o s) w d", w=2),
                        ps[ACC[q % 2]][:, :].rearrange("p (w s d) -> p s w d", w=2, s=HI), ACT.Copy)\
                        .then_inc(A_ready, 1)

            act.wait_ge(flag_set, 1)
            slow = act.value_load(flag[0:1, 0:1], min_val=0, max_val=1)
            with act.If(slow == 1):
                with act.Fori(0, T) as i:
                    with act.Fori(0, WT) as u:
                        act.wait_ge(sl_win, i * WT + u + 1)
                        act.activation(A4[:, ds(i, 1), :, ds(u * WIN, WIN)].rearrange("p o s d -> p (o s) d"),
                                       ps[ACC[0]][:, 0:KEY].rearrange("p (s d) -> p s d", s=HI), ACT.Copy)\
                            .then_inc(sl_A, 1)

            with act.Fori(0, B) as b:
                for k in range(K):
                    act.wait_ge(z1_done, b * K + k + 1)
                    act.activation(H1[:, ds(b, 1), k, :], ps[GZ[k]][:, :], ACT.Relu,
                                   bias=bias1[:, k:k + 1], scale=iS1).then_inc(h1_ready, 1)
            def split_high(c):
                for j in range(TB):
                    act.wait_ge(c_lo, c * TB + TB)
                    act.activation(H5[:, ds(c * -TB + (B * TB + j), 1), 0].rearrange("p o k n -> p (o k) n"),
                                   H1[:, ds(c * -1 + (B - 1), 1), :, j * P:(j + 1) * P].rearrange("p o k n -> p (o k) n"),
                                   ACT.Copy, scale=sHs).then_inc(c_hi, 1)

            def y_high(c):
                for j in range(TB):
                    act.wait_ge(y2_done, c * TB + j + 1)
                    act.activation(Y4[:, ds(c * -TB + ((B - 1) * TB + j), 1), 0, :], ps[GY[j % 2]][:, :], ACT.Copy)\
                        .then_inc(y2_hi, 1)

            act.wait_ge(sH_ready, 1)
            split_high(0)
            with act.Fori(0, B - 1) as c:
                split_high(c + 1)
                y_high(c)
            y_high(B - 1)
            with act.Fori(0, B) as b:
                for j in range(TB):
                    act.wait_ge(o_ready, b * TB + j + 3)
                    act.dma_start(out_p[:, ds(b * TB + j, 1), :].rearrange("p o f -> p (o f)"), ho[j % 2])\
                        .then_inc(o_out[j % 2], 16)
            for j in range(2):
                act.wait_ge(o_out[j], 16 * (T // 2) + 16)

        @block.vector
        def _(dve):
            count = [0]

            def link(ins):
                count[0] += 1
                ins.then_inc(dve_chain, 1)
                dve.wait_ge(dve_chain, count[0])

            def layernorm(t):
                dve.wait_ge(x_in[t % 3], 16 * (t // 3 + 1))
                link(dve.bn_stats(st6[:, :], xb[:, t % 3, :]))
                link(dve.bn_aggr(mv, st6[:, :]))
                dve.tensor_scalar(uvar, mv[:, 1:2], EPS, 0.25 / SH ** 2, ALU.add, ALU.mult).then_inc(var_ready, 1)
                dve.wait_ge(sd_ready, t + 1)
                link(dve.reciprocal(rinv, sd))
                link(dve.scalar_tensor_tensor(rinv, rinv, uvar, sd, ALU.mult, ALU.add))
                if t >= 2:
                    dve.wait_ge(h_f32, t - 1)
                r, n = rs[:, t % 2:t % 2 + 1], nb[:, t % 2:t % 2 + 1]
                link(dve.reciprocal(r, rinv))
                dve.tensor_scalar(n, mv[:, 0:1], r, -1.0, ALU.mult, ALU.mult).then_inc(norm_ready, 1)

            def exponent(v, bits_of_scale, scale, bits_of_inverse, inverse):
                link(dve.tensor_scalar(pint.bitcast(f32), v, 2.0 ** -60, None, ALU.max))
                link(dve.tensor_scalar(ebits, pint, 0x7F800000, None, ALU.bitwise_and))
                link(dve.tensor_scalar(inverse.bitcast(i32), ebits, float(bits_of_inverse << 23), None, ALU.subtract))
                return dve.tensor_scalar(scale.bitcast(i32), ebits, -1.0, float(bits_of_scale << 23), ALU.mult, ALU.add)

            def weight_max(l, t):
                dve.wait_ge(fold_copied, l * 2 * K + t + 1)
                link(dve.tensor_reduce(wmax[:, t:t + 1], Wf[:, l, t, :], X, ALU.max, apply_absolute_value=True))

            def weight_scale(l):
                link(dve.tensor_reduce(wtop, wmax, X, ALU.max))
                dve.sem_inc(wmax_ready, 1)
                dve.wait_ge(wall_ready, l + 1)
                exponent(wall, 255, sW[l], 1, iW[l]).then_inc(sW_ready, 1)
                dve.wait_ge(sW_ready, l + 1)

            def weight_low(l):
                for c in range(2):
                    dve.wait_ge(w_hi, l * 2 + c + 1)
                    ins = dve.scalar_tensor_tensor(Wb[:, l, c, 1], Wf[:, l, c * K:(c + 1) * K, :], sW[l], Wb[:, l, c, 0],
                                                   ALU.mult, ALU.subtract)
                ins.then_inc(w_lo, 1)

            def onehots(i):
                for h in range(2):
                    dve.wait_ge(pair_done, i * (WT // 2) + 2 * h + 2)
                    for v, c, n in ((1, 0, P), (0, P, KEY)):
                        rows = keyT[:, v, ds(i * ST + h * (ST // 2), ST // 2)].rearrange("p (g r) -> p g r", r=SIDE)
                        ins = dve.tensor_tensor(
                            R4[:, h * HG:(h + 1) * HG, c:c + n, :],
                            iota4[:, 0:n, :].unsqueeze(1).to_broadcast([P, HG, n, SIDE]),
                            rows.unsqueeze(2).to_broadcast([P, HG, n, SIDE]), ALU.is_equal)
                    ins.then_inc(onehot_ready, 1)

            dve.sem_inc(sl_oh, 1)
            dve.sem_inc(o_ready, 2)
            dve.wait_ge(dst_in, 16)
            link(dve.tensor_scalar(bit1, dnat, 7, None, ALU.logical_shift_right))
            link(dve.tensor_scalar(bit0, dnat, 4, 7, ALU.logical_shift_right, ALU.bitwise_and))
            dve.wait_ge(consts, 8)
            dve.tensor_tensor(oh1, bit1.unsqueeze(2).to_broadcast([P, EC, 16]),
                              iota16[:, 0:16].unsqueeze(1).to_broadcast([P, EC, 16]), ALU.is_equal)
            dve.tensor_tensor(oh0, bit0.unsqueeze(2).to_broadcast([P, EC, 8]),
                              iota16[:, 0:8].unsqueeze(1).to_broadcast([P, EC, 8]), ALU.is_equal).then_inc(oh_hist, 1)
            link(dve.tensor_scalar(pint, pidx, 15, None, ALU.bitwise_and))
            link(dve.tensor_scalar(b1off, pint, 8.0, None, ALU.mult))
            link(dve.tensor_scalar(before, wminus, b1off, None, ALU.is_gt))
            layernorm(0)
            layernorm(1)
            dve.wait_ge(hist_done, 1)
            link(dve.tensor_tensor(masked, ps[MISC][:, 0:HB * 8].rearrange("p (c b) -> p c b", c=HB), delta[:, :, :], ALU.mult))
            dve.tensor_reduce(hist, masked.rearrange("p c b -> p b c"), X, ALU.add).then_inc(hist_ready, 1)
            layernorm(2)
            layernorm(3)
            dve.wait_ge(start_done, 1)
            dve.tensor_scalar(start, ps[MISC][:, 64:65], float(E - CAP), None, ALU.min).then_inc(start_ready, 1)
            layernorm(4)
            layernorm(5)
            dve.wait_ge(dst_g, 16)
            link(dve.tensor_scalar(rel, dstw, wbase, None, ALU.subtract))
            link(dve.tensor_scalar(bad, rel, 0.0, None, ALU.is_lt))
            link(dve.scalar_tensor_tensor(bad, rel, float(WIN), bad, ALU.is_ge, ALU.add))
            link(dve.tensor_reduce(badsum, bad, X, ALU.add))
            link(dve.scalar_tensor_tensor(key, bad, FAR, rel, ALU.mult, ALU.add))
            dve.wait_ge(src_g, 16)
            link(dve.tensor_scalar(highi, srcw, 3, 0x7F0, ALU.logical_shift_right, ALU.bitwise_and))
            link(dve.tensor_scalar(lowi, srcw, P - 1, None, ALU.bitwise_and))
            link(dve.tensor_tensor(key, key, highi, ALU.add))
            dve.tensor_copy(low, lowi).then_inc(keys_ready, 1)
            dve.wait_ge(keyT_done, 1)
            for v in range(2):
                dve.tensor_copy(keyT[:, v, :].rearrange("p (w j) -> p w j", j=CH),
                                ps[v][:, 0:CH * P].rearrange("p (j w) -> p w j", j=CH)).then_inc(keyT_copied, 1)
            dve.wait_ge(cover_done, 1)
            dve.tensor_scalar(flag, ps[MISC][:, 66:67], float(CAP * P - E), None, ALU.not_equal).then_inc(flag_set, 1)
            for t in range(6, 9):
                layernorm(t)
            for t in range(2 * K):
                weight_max(0, t)
            weight_scale(0)
            layernorm(9)
            layernorm(10)
            weight_low(0)
            for t in range(11, T):
                layernorm(t)
            onehots(0)
            dve.tensor_scalar(iS1, iW[0], 1 / SH, None, ALU.mult)
            dve.wait_ge(b_in, 48)
            dve.tensor_copy(bcol[:, :, :], brel[:, K:2 * K].unsqueeze(2).to_broadcast([P, K, P])).then_inc(bcol_ready, 1)
            dve.wait_ge(b1_done, 1)
            dve.tensor_tensor(bias1, ps[MISC][:, P:P + K], blin, ALU.add).then_inc(b1_ready, 1)
            for t in range(2 * K):
                weight_max(1, t)
            weight_scale(1)
            weight_low(1)
            dve.wait_ge(b2_done, 1)
            dve.tensor_copy(bias2[:, :], ps[MISC][:, :]).then_inc(b2_ready, 1)

            with dve.Fori(0, T - 1) as i:
                onehots(i + 1)

            slow = dve.value_load(flag[0:1, 0:1], min_val=0, max_val=1)
            with dve.If(slow == 1):
                dve.wait_ge(sl_in, 32)
                dve.tensor_scalar(s_lowi, s_src, P - 1, None, ALU.bitwise_and).then_inc(sl_chain, 1)
                dve.wait_ge(sl_chain, 1)
                dve.tensor_copy(s_low, s_lowi).then_inc(sl_chain, 1)
                dve.tensor_scalar(s_high, s_src, 3, 0x7F0, ALU.logical_shift_right, ALU.bitwise_and).then_inc(sl_chain, 1)
                dve.tensor_copy(s_rel, s_dst).then_inc(sl_chain, 1)
                dve.wait_ge(sl_chain, 4)
                with dve.Fori(0, T) as i:
                    with dve.Fori(0, WT) as u:
                        w = i * WT + u
                        c = 4 + w * 5
                        dve.tensor_scalar(s_tmp, s_rel, 0.0, None, ALU.is_lt).then_inc(sl_chain, 1)
                        dve.wait_ge(sl_chain, c + 1)
                        dve.scalar_tensor_tensor(s_tmp, s_rel, float(WIN), s_tmp, ALU.is_ge, ALU.add).then_inc(sl_chain, 1)
                        dve.wait_ge(sl_chain, c + 2)
                        dve.wait_ge(sl_oh, w * EC + 1)
                        dve.scalar_tensor_tensor(s_key, s_tmp, FAR, s_rel, ALU.mult, ALU.add).then_inc(sl_chain, 1)
                        dve.wait_ge(sl_chain, c + 3)
                        dve.tensor_tensor(s_key, s_key, s_high, ALU.add).then_inc(sl_chain, 1)
                        dve.tensor_scalar(s_rel, s_rel, -float(WIN), None, ALU.add).then_inc(sl_chain, 1)
                        with dve.Fori(0, EC // 2) as m:
                            for h in range(2):
                                dve.wait_ge(sl_chain, c + 5)
                                dve.wait_ge(sl_free, w * EC + 2 * m + h + 1)
                                dve.tensor_scalar(s_oh[h][:, 0:P], iota16[:, 0:P], s_low[:, ds(2 * m + h, 1)], None,
                                                  ALU.is_equal)
                                dve.tensor_scalar(s_oh[h][:, P:OH], iota16[:, :], s_key[:, ds(2 * m + h, 1)], None,
                                                  ALU.is_equal).then_inc(sl_oh, 1)
                        dve.wait_ge(sl_A, w + 1)
                        dve.wait_ge(sl_st, 16 * i + 16)
                        dve.tensor_tensor(A2s[:, :, ds(u * WIN, WIN)],
                                          ps[ACC[0]][:, 0:KEY].rearrange("p (s d) -> p s d", s=HI),
                                          A4[:, ds(i, 1), :, ds(u * WIN, WIN)].rearrange("p o s d -> p (o s) d"),
                                          ALU.subtract).then_inc(sl_A2, 1)

            with dve.Fori(0, B) as b:
                for k in range(K):
                    dve.wait_ge(h1_ready, b * K + k + 1 + K)
                    dve.tensor_reduce(hmax[:, ds(b * K + k, 1)], H1[:, ds(b, 1), k, :].rearrange("p o n -> p (o n)"),
                                      X, ALU.max).then_inc(hmax_part, 1)
            dve.wait_ge(hmax_part, B * K)
            link(dve.tensor_reduce(htop, hmax, X, ALU.max))
            dve.sem_inc(hmax_ready, 1)
            dve.wait_ge(hall_ready, 1)
            exponent(hall, 257, sHs, 3, iH).then_inc(sH_ready, 1)
            dve.wait_ge(sH_ready, 1)
            link(dve.tensor_tensor(iS2, iH, iW[1], ALU.mult))

            def split_low(c):
                for j in range(TB):
                    t = c * -TB + (B * TB + j)
                    dve.wait_ge(c_hi, c * TB + j + 1)
                    dve.scalar_tensor_tensor(
                        H5[:, ds(t, 1), 1].rearrange("p o k n -> p (o k) n"),
                        H1[:, ds(c * -1 + (B - 1), 1), :, j * P:(j + 1) * P].rearrange("p o k n -> p (o k) n"), sHs,
                        H5[:, ds(t, 1), 0].rearrange("p o k n -> p (o k) n"), ALU.mult, ALU.subtract).then_inc(c_lo, 1)

            def y_low(c):
                for j in range(TB):
                    n = c * -TB + ((B - 1) * TB + j)
                    dve.wait_ge(y2_hi, c * TB + j + 1)
                    dve.tensor_tensor(Y4[:, ds(n, 1), 1, :].rearrange("p o f -> p (o f)"), ps[GY[j % 2]][:, :],
                                      Y4[:, ds(n, 1), 0, :].rearrange("p o f -> p (o f)"), ALU.subtract).then_inc(y2_lo, 1)

            split_low(0)
            with dve.Fori(0, B - 1) as c:
                split_low(c + 1)
                y_low(c)
            y_low(B - 1)
            with dve.Fori(0, B) as b:
                for j in range(TB):
                    dve.wait_ge(z2_done, b * TB + j + 1)
                    dve.wait_ge(o_out[j % 2], (b * (TB // 2) + j // 2 + 1) * 16)
                    dve.scalar_tensor_tensor(ho[j % 2], ps[GZ[j]][:, :], iS2, bias2[:, :], ALU.mult, ALU.add)\
                        .then_inc(z2_read, 1)
                    dve.wait_ge(z2_read, b * TB + j + 1 + TB)
                    dve.wait_ge(xr_in[j % 2], (b * (TB // 2) + j // 2 + 1) * 16)
                    dve.scalar_tensor_tensor(ho[j % 2], ho[j % 2], 0.0, xb[:, j % 2, :], ALU.max, ALU.add)\
                        .then_inc(o_ready, 1)

        @block.tensor
        def _(pe):
            def transpose_lin(l):
                if l == 1:
                    pe.wait_ge(w_in[1][LIN], 16)
                    pe.wait_ge(keyT_copied, 2)
                for q in range(K):
                    if l == 0:
                        pe.wait_ge(lin_in[q], 16)
                    for k in range(K):
                        ins = pe.transpose(ps[WTB[k]][:, q * P:(q + 1) * P], raw[l][:, LIN, q, k * P:(k + 1) * P], ident[:, :])
                        if q == K - 1:
                            ins.then_inc(wt_done, 1)

            def fold(l, t):
                c, q = t // K, t % K
                if t % K == 0:
                    pe.wait_ge(w_in[l][c], 16)
                if t == 0:
                    pe.wait_ge(wt_copied, (l + 1) * K)
                g = l * 2 * K + t
                if g >= 2:
                    pe.wait_ge(fold_copied, g - 1)
                for k in range(K):
                    ins = pe.matmul(ps[FOLD[t % 2]][:, :], raw[l][:, c, k, q * P:(q + 1) * P], raw[l][:, LINT, k, :],
                                    start=(k == 0), stop=(k == K - 1))
                ins.then_inc(fold_done, 1)

            def transpose_h(t):
                pe.wait_ge(h_lo, t + 1)
                if t >= 1:
                    pe.wait_ge(hT_ready, t)
                for a in range(2):
                    for k in range(K):
                        ins = pe.transpose(tp16[:, a, k, :], hs[:, t % 2, a, k * P:(k + 1) * P], ident16[:, :])
                ins.then_inc(tp_done, 1)

            def split_products(out_, left, right):
                terms = [(k, a, b) for k in range(K) for a, b in ((0, 0), (0, 1), (1, 0))]
                return [(out_, left(k, a), right(k, b)) for k, a, b in terms]

            pe.sem_inc(pair_done, WT // 2)
            pe.sem_inc(y_f32, 1)
            pe.sem_inc(y_lo, 1)
            pe.wait_ge(consts, 8)
            transpose_lin(0)
            for t in range(2 * K):
                fold(0, t)
                if t == 1:
                    pe.wait_ge(oh_hist, 1)
                    for c in range(0, EC, HB):
                        ins = pe.matmul(ps[MISC][:, 0:HB * 8], oh1[:, c:c + HB, :].rearrange("p c v -> p (c v)"),
                                        oh0[:, c:c + HB, :].rearrange("p c v -> p (c v)"),
                                        start=(c == 0), stop=(c == EC - HB))
                    ins.then_inc(hist_done, 1)
                if t == 3:
                    pe.wait_ge(hist_ready, 1)
                    for b in range(8):
                        ins = pe.matmul(ps[MISC][:, 64:65], before[:, b, :], hist[:, b:b + 1], start=(b == 0), stop=(b == 7))
                    ins.then_inc(start_done, 1)
                transpose_h(t)
                if t == 5:
                    pe.wait_ge(keys_ready, 1)
                    for v, rows in enumerate((key, low)):
                        for j in range(CH):
                            ins = pe.transpose(ps[v][:, j * P:(j + 1) * P], rows[:, j * P:(j + 1) * P], ident[:, :])
                    ins.then_inc(keyT_done, 1)
                    pe.matmul(ps[MISC][:, 66:67], ones[:, :], badsum, start=True, stop=True).then_inc(cover_done, 1)
            pe.wait_ge(b_in, 48)
            for q in range(K):
                for k in range(K):
                    ins = pe.matmul(ps[MISC][:, P + q:P + q + 1], raw[0][:, LINT, k, q * P:(q + 1) * P], brel[:, k:k + 1],
                                    start=(k == 0), stop=(k == K - 1))
            ins.then_inc(b1_done, 1)
            transpose_lin(1)
            for t in range(2 * K):
                fold(1, t)
                transpose_h(2 * K + t)
            pe.wait_ge(bcol_ready, 1)
            pe.wait_ge(b1_ready, 1)
            pe.wait_ge(brow_in, 16)
            for k in range(K):
                pe.matmul(ps[MISC][:, :], bcol[:, k, :], raw[1][:, LINT, k, :], start=(k == 0), stop=False)
            pe.matmul(ps[MISC][:, :], ones[0:1, :], brow[0:1, :], start=False, stop=True).then_inc(b2_done, 1)

            pe.wait_ge(flag_set, 1)
            slow = pe.value_load(flag[0:1, 0:1], min_val=0, max_val=1)
            pe.wait_ge(w_lo, 1)
            pe.wait_ge(hT_ready, T)
            with pe.Fori(0, T) as i:
                pe.wait_ge(y_f32, i + 1)
                todo = split_products(ps[GY[0]][:, :], lambda k, a: H5[:, ds(i + TB, 1), a, k, :].rearrange("p o n -> p (o n)"),
                                      lambda k, b: Wb[:, 0, 0, b, k, :])
                for n, (o_, l_, r_) in enumerate(todo):
                    ins = pe.matmul(o_, l_, r_, start=(n == 0), stop=(n == len(todo) - 1))
                ins.then_inc(y_done, 1)
                for u in range(WT):
                    if u % 2 == 0:
                        pe.wait_ge(A_ready, i * (WT // 2) + u // 2 + 1)
                    if u % (WT // 2) == 0:
                        pe.wait_ge(onehot_ready, i * 2 + u // (WT // 2) + 1)
                    for j in range(CH):
                        g, r = divmod(u * CH + j, SIDE)
                        ins = pe.matmul(ps[ACC[u // 2 % 2]][:, u % 2 * KEY:(u % 2 + 1) * KEY], R4[:, g, 0:P, r], R4[:, g, P:OH, r],
                                        start=(j == 0), stop=(j == CH - 1))
                    if u % 2 == 1:
                        ins.then_inc(pair_done, 1)

            with pe.If(slow == 1):
                pe.wait_ge(A_ready, T * WT // 2 + 2)
                pe.sem_inc(sl_free, 2)
                pe.sem_inc(a2_used, 1)
                pe.sem_inc(sl_A2, 1)
                with pe.Fori(0, T * WT) as w:
                    pe.wait_ge(sl_A2, w + 1)

                    def pair(chunk, first, last):
                        for h in range(2):
                            pe.wait_ge(sl_oh, chunk + h + 2)
                            ins = pe.matmul(ps[ACC[0]][:, 0:KEY], s_oh[h][:, 0:P], s_oh[h][:, P:OH],
                                            start=first and h == 0, stop=last and h == 1)
                            ins.then_inc(sl_free, 1)

                    pair(w * EC, True, False)
                    with pe.Fori(1, EC // 2 - 1) as m:
                        pair(w * EC + 2 * m, False, False)
                    pair(w * EC + EC - 2, False, True)
                    pe.wait_ge(sl_free, w * EC + EC + 2)
                    pe.sem_inc(sl_win, 1)
                pe.wait_ge(sl_A2, T * WT + 1)

            with pe.Fori(0, B) as b:
                for q in range(K):
                    z = ps[GZ[q]][:, :].rearrange("p (t n) -> p t n", t=TB)
                    cols = slice(q * P, (q + 1) * P)
                    pe.wait_ge(h1_ready, b * K + q + 1)
                    todo = split_products(z, lambda k, a: Wb[:, 0, 1, a, k, cols], lambda k, c: H5[:, ds(b * TB + TB, TB), c, k, :])
                    for n, (o_, l_, r_) in enumerate(todo):
                        pe.matmul(o_, l_, r_, start=(n == 0), stop=False)
                    pe.wait_ge(y_lo, T + 1)
                    pe.wait_ge(A_ready, T * WT // 2 + 2)
                    with pe.If(slow == 1):
                        pe.wait_ge(a2_in, 16 * b + 16)
                        for s in range(HI):
                            for a in range(2):
                                pe.matmul(z, Y4[:, s, a, cols], A2[:, :, s, :], start=False, stop=False)
                    for s in range(HI):
                        for a in range(2):
                            ins = pe.matmul(z, Y4[:, s, a, cols], A4[:, ds(b * TB, TB), s, :],
                                            start=False, stop=(s == HI - 1 and a == 1))
                    ins.then_inc(z1_done, 1)
                with pe.If(slow == 1):
                    pe.drain().then_inc(a2_used, 1)

            pe.sem_inc(y2_lo, 2)
            pe.sem_inc(z2_read, TB)
            with pe.Fori(0, B) as c:
                for j in range(TB):
                    pe.wait_ge(c_lo, c * TB + j + 1 + TB)
                    pe.wait_ge(y2_lo, c * TB + j + 1)
                    todo = split_products(ps[GY[j % 2]][:, :],
                                          lambda k, a: H5[:, ds(c * -TB + (B * TB + j), 1), a, k, :].rearrange("p o n -> p (o n)"),
                                          lambda k, b: Wb[:, 1, 0, b, k, :])
                    for n, (o_, l_, r_) in enumerate(todo):
                        ins = pe.matmul(o_, l_, r_, start=(n == 0), stop=(n == len(todo) - 1))
                    ins.then_inc(y2_done, 1)

            with pe.Fori(0, B) as b:
                for j in range(TB):
                    z = ps[GZ[j]][:, :]
                    pe.wait_ge(z2_read, b * TB + j + 1)
                    todo = split_products(z, lambda k, a: H5[:, ds((b + 1) * TB + j, 1), a, k, :].rearrange("p o n -> p (o n)"),
                                          lambda k, c: Wb[:, 1, 1, c, k, :])
                    for n, (o_, l_, r_) in enumerate(todo):
                        pe.matmul(o_, l_, r_, start=(n == 0), stop=False)
                    pe.wait_ge(y2_lo, T + 2)
                    with pe.If(slow == 1):
                        pe.wait_ge(a2_in, 16 * b + 16 * B + 16)
                        for s in range(HI):
                            for a in range(2):
                                pe.matmul(z, A2[:, j, s, :], Y4[:, s, a, :], start=False, stop=False)
                    for s in range(HI):
                        for a in range(2):
                            ins = pe.matmul(z, A4[:, ds(b * TB + j, 1), s, :].rearrange("p o n -> p (o n)"), Y4[:, s, a, :],
                                            start=False, stop=(s == HI - 1 and a == 1))
                    ins.then_inc(z2_done, 1)
                with pe.If(slow == 1):
                    pe.drain().then_inc(a2_used, 1)


_INS = ["x", "src", "dst"] + [f"L0_gnn_{n}" for n in ("W_rel1", "b_rel1", "W_root1", "W_lin1", "b_lin1",
                                                     "W_rel2", "b_rel2", "W_root2", "W_lin2", "b_lin2")]


def kernel(**inputs):
    import numpy as _np
    import concourse.bacc as _bacc
    from concourse import mybir as _mybir
    from concourse.bass_utils import run_bass_kernel_spmd as _run

    nc = _bacc.Bacc("TRN2", target_bir_lowering=False, num_devices=1)
    arrays, args = {}, []
    for name in _INS:
        a = _np.ascontiguousarray(inputs[name])
        arrays[f"in_{name}"] = a
        args.append(nc.dram_tensor(f"in_{name}", a.shape, _mybir.dt.from_np(a.dtype), kind="ExternalInput").ap())
    out = nc.dram_tensor("out_0", inputs["x"].shape, _mybir.dt.float32, kind="ExternalOutput").ap()
    gnn_block_kernel(nc, *args, out)
    return _run(nc, [arrays], core_ids=[0]).results[0]["out_0"]
```

```python
import numpy as np
import concourse.bass as bass
from concourse import mybir
from contextlib import ExitStack


def gnn_block_kernel(nc, x, src, dst, W_rel1, b_rel1, W_root1, W_lin1, b_lin1,
                     W_rel2, b_rel2, W_root2, W_lin2, b_lin2, out):
    f32, f16 = mybir.dt.float32, mybir.dt.float16
    i32, u32 = mybir.dt.int32, mybir.dt.uint32
    ALU = mybir.AluOpType
    ACT = mybir.ActivationFunctionType
    X = mybir.AxisListType.X
    ds = bass.ds

    P = 128
    N, F = x.shape
    E = src.shape[0]
    T = N // P
    K = F // P
    B = 4
    TB = T // B
    NB = N // B
    WIN = N // P
    WT = P // WIN
    HI = N // P
    KEY = HI * WIN
    CH = 3
    CAP = CH * P
    EC = E // P
    OH = P + KEY
    ST = WT * CH
    SIDE = 4
    HG = ST // 2 // SIDE
    HB = 8
    FAR = 4096.0
    EPS = 1e-5
    SH = 16.0
    REL, ROOT, LIN, LINT = range(4)
    assert K == 4 and N == WIN * P and HI * WIN == KEY and E == EC * P and KEY == 256 and EC % HB == 0

    at2_dram = nc.dram_tensor("at2", (T, P, HI * P), f16, kind="Internal").ap()
    x_t = x.rearrange("(t p) f -> t p f", p=P)
    x_p = x.rearrange("(t p) f -> p t f", p=P)
    out_p = out.rearrange("(t p) f -> p t f", p=P)

    ctx = ExitStack()
    with ctx:
        def sb(name, shape, dt):
            return ctx.enter_context(nc.sbuf_tensor(name, shape, dt))

        def sem(name):
            return ctx.enter_context(nc.semaphore(name))

        At = sb("At", [P, T * HI * P], f16)
        A4 = At[:, :].rearrange("p (t s d) -> p t s d", t=T, s=HI)
        Yt = sb("Yt", [P, T * 2 * F], f16)
        Y4 = Yt[:, :].rearrange("p (t a f) -> p t a f", t=T, a=2)
        Ht = sb("Ht", [P, (B + 1) * TB * 2 * K * P], f16)
        H5 = Ht[:, :].rearrange("p (t a k n) -> p t a k n", a=2, k=K, n=P)
        Hf = Ht[:, :].bitcast(f32)
        H1 = Hf.rearrange("p (b k n) -> p b k n", b=B + 1, k=K)
        Wb = sb("Wb", [P, 2, 2, 2, K, F], f16)
        ring = sb("ring", [P, ST * OH], f16)
        R4 = ring[:, :].rearrange("p (g c r) -> p g c r", c=OH, r=SIDE)
        last = sb("last", [P, 4, F], f32)
        xb, ot = last[:, 0:2], last[:, 2:4]
        yf = sb("yf", [P, F], f32)
        bias2 = sb("bias2", [P, F], f32)
        ident = sb("ident", [P, P], f32)
        ones = sb("ones", [P, P], f32)
        iota4 = sb("iota4", [P, KEY, SIDE], f16)
        iota16 = iota4[:, :, 0]
        keyT = sb("keyT", [P, 2, P * CH], f16)
        delta = sb("delta", [P, 8, HB], f32)
        hist16 = sb("hist16", [P, 8, 2], f16)
        small = sb("small", [P, 176], f32)
        smi = sb("smi", [P, 16], i32)
        st6 = sb("st6", [P, TB, 6], f32)
        brow = sb("brow", [1, F], f32)
        bcol = sb("bcol", [P, K, P], f32)

        RW, FW = 4 * K * F, 2 * K * F
        Af = At[:, :].bitcast(f32)
        raw = [v.rearrange("p (w k f) -> p w k f", w=4, k=K) for v in (Yt[:, :].bitcast(f32), Af[:, FW:FW + RW])]
        Wf = [v.rearrange("p (t f) -> p t f", t=2 * K) for v in (Af[:, 0:FW], Af[:, FW + RW:])]
        lint = [raw[0][:, LINT], last]
        H_TILE = K * P

        def part(base, at, n, dt):
            v = base[:, at:at + n]
            return v if dt == f32 else v.bitcast(dt)

        srcw, dstw, rel, bad, key = [part(Hf, i * CAP, CAP, dt) for i, dt in enumerate((i32, i32, f32, f32, f32))]
        SL = TB * K * P
        oh1 = Hf[:, 3 * SL:3 * SL + EC * 8].bitcast(f16).rearrange("p (g v c) -> p g v c", v=16, c=HB)
        oh0 = Hf[:, 3 * SL + EC * 8:3 * SL + EC * 12].bitcast(f16).rearrange("p (g v c) -> p g v c", v=8, c=HB)
        bits = Hf[:, 3 * SL + EC * 12:3 * SL + EC * 13].bitcast(f16).rearrange("p (v g c) -> p v g c", v=2, c=HB)
        rf = ring[:, :].bitcast(f32)
        before = ring[:, 0:8 * P].rearrange("p (b w) -> p b w", b=8)
        wminus = rf[:, 8 * P:16 * P].rearrange("p (b w) -> p b w", b=8)
        dnat, bit1, bit0 = [part(rf, 16 * P + i * EC, EC, i32) for i in range(3)]
        o = 16 * P + 3 * EC
        lowi, highi, low = part(rf, o, CAP, i32), part(rf, o + CAP, CAP, i32), part(rf, o + 2 * CAP, CAP, f32)
        masked = key[:, 0:HB * 8].rearrange("p (b c) -> p b c", c=HB)

        def x_of(t):
            return Hf[:, (t + TB) * H_TILE:(t + TB + 1) * H_TILE]

        s_src, s_dst, s_low, s_high, s_rel, s_key, s_tmp = [
            part(Hf, i * EC, EC, dt) for i, dt in enumerate((i32, i32, f32, i32, f32, f32, f32))]
        s_lowi = s_tmp.bitcast(i32)
        s_oh = [ring[:, i * OH:(i + 1) * OH] for i in range(2)]
        A2s = ring[:, 2 * OH:2 * OH + HI * P].rearrange("p (s d) -> p s d", s=HI)
        A2 = ring[:, 0:TB * HI * P].rearrange("p (t s d) -> p t s d", t=TB, s=HI)

        at = [0]

        def col(n):
            at[0] += n
            return small[:, at[0] - n:at[0]]

        hist, wbase, b1off, cmod, startf = col(8), col(1), col(1), col(1), col(1)
        badsum, mv, sd, rs, nb, uvar, rinv = col(1), col(2 * TB), col(TB), col(T), col(T), col(TB), col(TB)
        mv2 = mv.rearrange("p (t v) -> p t v", v=2)
        wmax, wtop, wall, brel2, blin, bias1 = col(2 * K), col(1), col(1), col(K), col(K), col(K)
        sW = [col(1), col(1)]
        iW = [col(1), col(1)]
        hmax, htop, hall, sHs, iH, iS1, iS2 = col(B * K), col(1), col(1), col(1), col(1), col(1), col(1)
        start, pint, flag, ebits, pidx = smi[:, 0:1], smi[:, 1:2], smi[:, 2:3], smi[:, 3:4], smi[:, 4:5]

        ps = [ctx.enter_context(nc.psum_tensor(f"ps{i}", [P, F], f32)) for i in range(8)]
        ACC = (0, 1)
        TP = (2, 7)
        GY = (3, 4)
        FOLD = (5, 6)
        MISC = 4
        BIAS = 7
        GZ = (5, 6, 0, 1)
        WTB = ((0, 1, 2, 3), (0, 1, 3, 4))

        T_AFTER = {2: [0], 3: [1], 4: [2], 5: [3, 4], 6: [5], 7: [6], 8: [7],
                   9: [8], 10: [9, 10], 11: [11], 12: [12, 13], 13: [14], 14: [15]}
        RELU_AT = {0: [2, 3], 1: [4], 2: [5], 3: [6], 4: [7], 5: [8], 6: [9, 10], 7: [11], 8: [12, 13], 9: [14], 10: [15]}
        SQRT_AT = {1: 1, 4: 2, 7: 3}
        HIST_AT, START_AT, EDGES_AT, KEYS_AT = 0, 1, 6, 9
        STATS_AT = {2: [8, 9], 3: [10, 11], 4: [12, 13], 5: [14, 15]}
        ONEHOTS_AT = {11: 0, 13: 1}
        SPLIT_AT = {10: 0, 12: 1}

        dst_in, brow_in, b_in, brel1_in = sem("dst_in"), sem("brow_in"), sem("b_in"), sem("brel1_in")
        w_in = [[sem(f"w_in{l}{w}") for w in range(3)] for l in range(2)]
        lin_in = [sem(f"lin_in{q}") for q in range(K)]
        x_in = [sem(f"x_in{i}") for i in range(T)]
        rel_in = [sem(f"rel_in{q}") for q in range(K)]
        src_g, dst_g = sem("src_gathered"), sem("dst_gathered")
        consts, iotas = sem("consts"), sem("iotas")
        pool_chain, dve_chain = sem("pool_chain"), sem("dve_chain")
        wt_done, wt_copied = sem("wt_done"), sem("wt_copied")
        fold_done, fold_copied = sem("fold_done"), sem("fold_copied")
        oh_hist, hist_done, hist_ready, start_done, start_ready = [
            sem(n) for n in ("hist_onehots", "hist_done", "hist_ready", "start_done", "start_ready")]
        keys_ready, keyT_done, cover_done, flag_set = [sem(n) for n in ("keys_ready", "keyT_done", "cover_done", "flag_set")]
        hmax_part = sem("hmax_part")
        keyT_copied = sem("keyT_copied")
        var_ready, sd_ready, norm_ready = sem("var_ready"), sem("sd_ready"), sem("norm_ready")
        h_f32, tp_done, hT_hi, hT_lo = sem("h_f32"), sem("tp_done"), sem("hT_hi"), sem("hT_lo")
        ident_ready, w2_hi, w2_lo, w2_scaled = [sem(n) for n in ("ident_ready", "w2_hi", "w2_lo", "w2_scaled")]
        wmax_ready, wall_ready, sW_ready, w_hi, w_lo = [sem(n) for n in ("wmax_ready", "wall_ready", "sW_ready", "w_hi", "w_lo")]
        b1_done, b1_ready, bcol_ready, b2_done, b2_ready = [sem(n) for n in ("b1_done", "b1_ready", "bcol_ready", "b2_done", "b2_ready")]
        onehot_ready, pair_done = sem("onehot_ready"), sem("pair_done")
        A_ready = sem("A_ready")
        y_done, y_f32, y_hi, y_lo = sem("y_done"), sem("y_f32"), sem("y_hi"), sem("y_lo")
        z1_done, h1_ready, hmax_ready, hall_ready, sH_ready = [
            sem(n) for n in ("z1_done", "h1_ready", "hmax_ready", "hall_ready", "sH_ready")]
        c_hi, c_lo = sem("c_hi"), sem("c_lo")
        y2_done, y2_hi, y2_lo = sem("y2_done"), sem("y2_hi"), sem("y2_lo")
        z2_done, z2_read, o_ready = sem("z2_done"), sem("z2_read"), sem("o_ready")
        xr_in = [sem(f"xr_in{i}") for i in range(2)]
        o_out = [sem(f"o_out{i}") for i in range(2)]
        sl_in, sl_oh, sl_free, sl_win, sl_A, sl_A2, sl_st, sl_chain = [
            sem(n) for n in ("slow_in", "slow_onehot", "slow_free", "slow_window", "slow_A", "slow_A2", "slow_stored", "slow_chain")]
        a2_in, a2_used = sem("a2_in"), sem("a2_used")

        block = ctx.enter_context(nc.Block())

        @block.sync
        def _(sp):
            W = ((W_rel1, W_root1, W_lin1), (W_rel2, W_root2, W_lin2))

            def load_w(l, w):
                sp.dma_start(raw[l][:, w], W[l][w].rearrange("(k p) f -> p k f", p=P)).then_inc(w_in[l][w], 16)

            def load_x(t):
                sp.dma_start(x_of(t), x_t[t]).then_inc(x_in[t], 16)

            sp.dma_start(dnat, dst.rearrange("(p c) -> p c", p=P)).then_inc(dst_in, 16)
            for w, d, sems in ((LIN, W_lin1, lin_in), (REL, W_rel1, rel_in)):
                for q in range(K):
                    cols = slice(q * P, (q + 1) * P)
                    sp.dma_start(raw[0][:, w, :, cols], d.rearrange("(k p) f -> p k f", p=P)[:, :, cols])\
                        .then_inc(sems[q], 16)
            for t in range(2 * TB):
                load_x(t)
            load_w(0, ROOT)
            for v, d in ((brel2, b_rel2), (blin, b_lin1)):
                sp.dma_start(v, d.rearrange("(k p) -> p k", p=P), allow_slow_non_contiguous=True).then_inc(b_in, 16)
            sp.dma_start(brow[:, :], b_lin2.rearrange("(a f) -> a f", a=1)).then_inc(brow_in, 16)
            sp.dma_start(yf[:, :], b_rel1.rearrange("(a f) -> a f", a=1).to_broadcast([P, F])).then_inc(brel1_in, 16)
            sp.wait_ge(hist_done, 1)
            for t in range(2 * TB, T):
                load_x(t)
            load_w(1, LIN)
            load_w(1, REL)
            load_w(1, ROOT)

            sp.sem_inc(sl_st, 16)
            sp.wait_ge(flag_set, 1)
            slow = sp.value_load(flag[0:1, 0:1], min_val=0, max_val=1)
            with sp.If(slow == 1):
                sp.wait_ge(A_ready, T * WT // 2 + 2)
                sp.dma_start(s_src, src.rearrange("(p c) -> p c", p=P)).then_inc(sl_in, 16)
                sp.dma_start(s_dst, dst.rearrange("(p c) -> p c", p=P)).then_inc(sl_in, 16)
                with sp.Fori(0, T) as i:
                    sp.wait_ge(sl_A2, (i + 1) * WT + 1)
                    sp.dma_start(at2_dram[ds(i, 1)].rearrange("o p n -> (o p) n"),
                                 A2s.rearrange("p s d -> p (s d)")).then_inc(sl_st, 16)
                sp.wait_ge(sl_st, 16 * T + 16)
                with sp.Fori(0, B) as b:
                    sp.wait_ge(a2_used, b + 1)
                    sp.dma_start(A2.rearrange("p t s d -> p t (s d)"),
                                 at2_dram[ds(b * TB, TB)].rearrange("t p n -> p t n")).then_inc(a2_in, 16)
            sp.wait_ge(b2_done, 1)
            with sp.Fori(0, B) as b:
                with sp.If(slow == 1):
                    sp.wait_ge(a2_used, b + B + 1)
                    sp.dma_start(A2.rearrange("p t s d -> p t (s d)"),
                                 at2_dram[ds(b * TB, TB)].rearrange("t p n -> p t n")).then_inc(a2_in, 16)
                for j in range(TB):
                    sp.wait_ge(o_ready, b * TB + j + 1)
                    sp.dma_start(xb[:, j % 2, :], x_p[:, ds(b * TB + j, 1), :].rearrange("p o f -> p (o f)"))\
                        .then_inc(xr_in[j % 2], 16)

        @block.gpsimd
        def _(pool):
            pool.memset(ident[:, :], 0.0).then_inc(pool_chain, 1)
            pool.wait_ge(pool_chain, 1)
            pool.affine_select(out=ident[:, :], in_=ident[:, :], compare_op=ALU.not_equal, fill=1.0, base=0,
                               pattern=[[-1, P]], channel_multiplier=1).then_inc(ident_ready, 1)
            pool.iota(pidx, pattern=[[0, 1]], base=0, channel_multiplier=1).then_inc(consts, 1)
            pool.iota(delta[:, :, :], pattern=[[0, 8], [1, HB]], base=0, channel_multiplier=0,
                      allow_small_or_imprecise_dtypes=True).then_inc(consts, 1)
            pool.iota(wminus, pattern=[[-1, 8], [1, P]], base=0, channel_multiplier=0,
                      allow_small_or_imprecise_dtypes=True).then_inc(consts, 1)
            pool.iota(wbase, pattern=[[0, 1]], base=0, channel_multiplier=WIN,
                      allow_small_or_imprecise_dtypes=True).then_inc(iotas, 1)
            pool.memset(ones[:, :], 1.0).then_inc(iotas, 1)
            pool.iota(iota4[:, :, :], pattern=[[1, KEY], [0, SIDE]], base=0, channel_multiplier=0,
                      allow_small_or_imprecise_dtypes=True).then_inc(iotas, 1)
            pool.wait_ge(start_ready, 1)
            for to, of, s in ((dstw, dst, dst_g), (srcw, src, src_g)):
                pool.indirect_dma_start(to, None, of.rearrange("(e o) -> e o", o=1),
                                        bass.IndirectOffsetOnAxis(start.bitcast(u32), 0)).then_inc(s, 16)
            for q in range(K):
                pool.wait_ge(lin_in[q], 16)
            pool.wait_ge(brel1_in, 16)
            pool.tensor_tensor(last[:, :, :], raw[0][:, LIN], yf[:, :].unsqueeze(1).to_broadcast([P, K, F]), ALU.mult)\
                .then_inc(b1_done, 1)
            for l in range(2):
                pool.wait_ge(wmax_ready, l + 1)
                pool.partition_all_reduce(wall, wtop, P, bass.bass_isa.ReduceOp.max).then_inc(wall_ready, 1)

            def y_low(i):
                pool.wait_ge(y_hi, i + 1)
                pool.tensor_tensor(Y4[:, ds(i, 1), 1, :].rearrange("p o f -> p (o f)"), yf[:, :],
                                   Y4[:, ds(i, 1), 0, :].rearrange("p o f -> p (o f)"), ALU.subtract).then_inc(y_lo, 1)

            pool.wait_ge(sW_ready, 2)
            for c in range(2):
                with pool.Fori(0, K) as k:
                    w = Wf[1][:, ds(k + c * K, 1), :].rearrange("p o f -> p (o f)")
                    y_low(k + c * K)
                    pool.wait_ge(w2_hi, k + c * K + 1)
                    pool.tensor_tensor(w, w, sW[1].to_broadcast([P, F]), ALU.mult).then_inc(w2_scaled, 1)
                    pool.wait_ge(w2_scaled, k + c * K + 1)
                    pool.tensor_tensor(Wb[:, 1, c, 1, ds(k, 1), :].rearrange("p o f -> p (o f)"), w,
                                       Wb[:, 1, c, 0, ds(k, 1), :].rearrange("p o f -> p (o f)"), ALU.subtract)\
                        .then_inc(w2_lo, 1)
            with pool.Fori(2 * K, T) as i:
                y_low(i)
            pool.wait_ge(hmax_ready, 1)
            pool.partition_all_reduce(hall, htop, P, bass.bass_isa.ReduceOp.max).then_inc(hall_ready, 1)

        @block.scalar
        def _(act):
            def wt_copies(l):
                for k in range(K):
                    act.wait_ge(wt_done, l * K + k + 1)
                    act.activation(lint[l][:, k, :], ps[WTB[l][k]][:, :], ACT.Copy).then_inc(wt_copied, 1)

            def square_root(b):
                act.wait_ge(var_ready, b + 1)
                act.activation(sd, uvar, ACT.Sqrt).then_inc(sd_ready, 1)

            def normalize(t):
                act.wait_ge(norm_ready, t // TB + 1)
                act.activation(x_of(t), x_of(t), ACT.Relu, bias=nb[:, t:t + 1], scale=rs[:, t:t + 1]).then_inc(h_f32, 1)

            def fold_copy(g):
                act.wait_ge(fold_done, g + 1)
                act.activation(Wf[g // (2 * K)][:, g % (2 * K), :], ps[FOLD[g % 2]][:, :], ACT.Copy).then_inc(fold_copied, 1)

            def h_high(t):
                act.wait_ge(tp_done, t + 1)
                act.activation(H5[:, t + TB, 0], ps[TP[t % 2]][:, :].rearrange("p (k n) -> p k n", k=K), ACT.Copy)\
                    .then_inc(hT_hi, 1)

            act.sem_inc(A_ready, 2)
            act.sem_inc(c_lo, TB)
            act.sem_inc(o_out[0], 16)
            act.sem_inc(o_out[1], 16)
            act.sem_inc(h1_ready, K)
            wt_copies(0)
            for g in range(T):
                if g == 2 * K - 1:
                    act.wait_ge(b1_ready, 1)
                    wt_copies(1)
                fold_copy(g)
                if g == 0:
                    square_root(0)
                    normalize(0)
                    normalize(1)
                if g in SQRT_AT:
                    square_root(SQRT_AT[g])
                for t in RELU_AT.get(g, ()):
                    normalize(t)
                for t in T_AFTER.get(g, ()):
                    h_high(t)
                if g in SPLIT_AT:
                    c = SPLIT_AT[g]
                    act.wait_ge(sW_ready, 1)
                    act.activation(Wb[:, 0, c, 0], Wf[0][:, c * K:(c + 1) * K, :], ACT.Copy, scale=sW[0]).then_inc(w_hi, 1)

            def tile(i):
                for q in range(WT // 2):
                    act.wait_ge(pair_done, i * (WT // 2) + q + 1 + WT // 2)
                    act.activation(A4[:, ds(i, 1), :, 2 * q * WIN:2 * (q + 1) * WIN].rearrange(
                        "p o s (w d) -> p (o s) w d", w=2),
                        ps[ACC[q % 2]][:, :].rearrange("p (w s d) -> p s w d", w=2, s=HI), ACT.Copy)\
                        .then_inc(A_ready, 1)
                    if q == 1:
                        act.wait_ge(y_done, i + 1)
                        act.wait_ge(y_lo, i + 1)
                        act.activation(yf[:, :], ps[GY[0]][:, :], ACT.Copy).then_inc(y_f32, 1)
                        act.wait_ge(y_f32, i + 2)
                        act.activation(Y4[:, ds(i, 1), 0, :], yf[:, :], ACT.Copy).then_inc(y_hi, 1)

            act.wait_ge(w_lo, 2)
            act.wait_ge(fold_done, 4 * K)
            for c in range(2):
                with act.Fori(0, K) as k:
                    tile(k + c * K)
                    act.wait_ge(sW_ready, 2)
                    act.activation(Wb[:, 1, c, 0, ds(k, 1), :], Wf[1][:, ds(k + c * K, 1), :], ACT.Copy, scale=sW[1])\
                        .then_inc(w2_hi, 1)
            with act.Fori(2 * K, T - TB) as i:
                tile(i)
            act.wait_ge(w2_lo, 2 * K)
            with act.Fori(T - TB, T) as i:
                tile(i)

            act.wait_ge(flag_set, 1)
            slow = act.value_load(flag[0:1, 0:1], min_val=0, max_val=1)
            with act.If(slow == 1):
                with act.Fori(0, T) as i:
                    with act.Fori(0, WT) as u:
                        act.wait_ge(sl_win, i * WT + u + 1)
                        act.activation(A4[:, ds(i, 1), :, ds(u * WIN, WIN)].rearrange("p o s d -> p (o s) d"),
                                       ps[ACC[0]][:, 0:KEY].rearrange("p (s d) -> p s d", s=HI), ACT.Copy)\
                            .then_inc(sl_A, 1)

            with act.Fori(0, B) as b:
                for k in range(K):
                    act.wait_ge(z1_done, b * K + k + 1)
                    act.activation(H1[:, ds(b, 1), k, :], ps[GZ[k]][:, :], ACT.Relu,
                                   bias=bias1[:, k:k + 1], scale=iS1).then_inc(h1_ready, 1)

            def split_high(c, j):
                act.wait_ge(c_lo, c * TB + TB)
                act.activation(H5[:, ds(c * -TB + (B * TB + j), 1), 0].rearrange("p o k n -> p (o k) n"),
                               H1[:, ds(c * -1 + (B - 1), 1), :, j * P:(j + 1) * P].rearrange("p o k n -> p (o k) n"),
                               ACT.Copy, scale=sHs).then_inc(c_hi, 1)

            def y_high(c, j):
                act.wait_ge(y2_done, c * TB + j + 1)
                act.activation(Y4[:, ds(c * -TB + ((B - 1) * TB + j), 1), 0, :], ps[GY[j % 2]][:, :], ACT.Copy)\
                    .then_inc(y2_hi, 1)

            act.wait_ge(sH_ready, 1)
            for j in range(TB):
                split_high(0, j)
            with act.Fori(0, B - 1) as c:
                for j in range(TB):
                    split_high(c + 1, j)
                    y_high(c, j)
            for j in range(TB):
                y_high(B - 1, j)
            with act.Fori(0, B) as b:
                for j in range(TB):
                    act.wait_ge(o_ready, b * TB + j + 3)
                    act.dma_start(out_p[:, ds(b * TB + j, 1), :].rearrange("p o f -> p (o f)"), ot[:, j % 2, :])\
                        .then_inc(o_out[j % 2], 16)
            for j in range(2):
                act.wait_ge(o_out[j], 16 * (T // 2) + 16)

        @block.vector
        def _(dve):
            count = [0]

            def link(ins):
                count[0] += 1
                ins.then_inc(dve_chain, 1)
                dve.wait_ge(dve_chain, count[0])

            def post(ins):
                count[0] += 1
                ins.then_inc(dve_chain, 1)

            def settle():
                dve.wait_ge(dve_chain, count[0])

            def statistics(*tiles):
                for t in tiles:
                    dve.wait_ge(x_in[t], 16)
                    post(dve.bn_stats(st6[:, t % TB, :], x_of(t)))
                settle()
                for t in tiles:
                    post(dve.bn_aggr(mv2[:, t % TB, :], st6[:, t % TB, :]))
                if t % TB == TB - 1:
                    settle()
                    dve.tensor_scalar(uvar, mv2[:, :, 1], EPS, 0.25 / SH ** 2, ALU.add, ALU.mult).then_inc(var_ready, 1)

            def norms(b):
                dve.wait_ge(sd_ready, b + 1)
                link(dve.reciprocal(rinv, sd))
                link(dve.tensor_tensor(rinv, rinv, uvar, ALU.mult))
                link(dve.tensor_tensor(rinv, rinv, sd, ALU.add))
                r, n = rs[:, b * TB:(b + 1) * TB], nb[:, b * TB:(b + 1) * TB]
                link(dve.reciprocal(r, rinv))
                link(dve.scalar_tensor_tensor(n, mv2[:, :, 0], -1.0, r, ALU.mult, ALU.mult))
                dve.sem_inc(norm_ready, 1)

            def h_low(t):
                dve.wait_ge(hT_hi, t + 1)
                dve.tensor_tensor(H5[:, t + TB, 1], ps[TP[t % 2]][:, :].rearrange("p (k n) -> p k n", k=K),
                                  H5[:, t + TB, 0], ALU.subtract).then_inc(hT_lo, 1)

            def exponent(v, bits_of_scale, scale, bits_of_inverse, inverse):
                link(dve.tensor_scalar(pint.bitcast(f32), v, 2.0 ** -60, None, ALU.max))
                link(dve.tensor_scalar(ebits, pint, 0x7F800000, None, ALU.bitwise_and))
                link(dve.tensor_scalar(inverse.bitcast(i32), ebits, float(bits_of_inverse << 23), None, ALU.subtract))
                return dve.tensor_scalar(scale.bitcast(i32), ebits, -1.0, float(bits_of_scale << 23), ALU.mult, ALU.add)

            def weight_max(l, t):
                dve.wait_ge(fold_copied, l * 2 * K + t + 1)
                post(dve.tensor_reduce(wmax[:, t:t + 1], Wf[l][:, t, :], X, ALU.max, apply_absolute_value=True))

            def weight_top(l):
                settle()
                link(dve.tensor_reduce(wtop, wmax, X, ALU.max))
                dve.sem_inc(wmax_ready, 1)

            def weight_scale(l):
                dve.wait_ge(wall_ready, l + 1)
                exponent(wall, 255, sW[l], 1, iW[l]).then_inc(sW_ready, 1)
                dve.wait_ge(sW_ready, l + 1)

            def weight_low(c):
                dve.wait_ge(w_hi, c + 1)
                dve.scalar_tensor_tensor(Wb[:, 0, c, 1], Wf[0][:, c * K:(c + 1) * K, :], sW[0], Wb[:, 0, c, 0],
                                         ALU.mult, ALU.subtract).then_inc(w_lo, 1)

            def onehots(i, h):
                dve.wait_ge(pair_done, i * (WT // 2) + 2 * h + 2)
                for v, c, n in ((1, 0, P), (0, P, KEY)):
                    rows = keyT[:, v, ds(i * ST + h * (ST // 2), ST // 2)].rearrange("p (g r) -> p g r", r=SIDE)
                    ins = dve.tensor_tensor(
                        R4[:, h * HG:(h + 1) * HG, c:c + n, :],
                        iota4[:, 0:n, :].unsqueeze(1).to_broadcast([P, HG, n, SIDE]),
                        rows.unsqueeze(2).to_broadcast([P, HG, n, SIDE]), ALU.is_equal)
                ins.then_inc(onehot_ready, 1)

            dve.sem_inc(sl_oh, 1)
            dve.sem_inc(o_ready, 2)
            dve.wait_ge(dst_in, 16)
            link(dve.tensor_scalar(bit1, dnat, 7, None, ALU.logical_shift_right))
            link(dve.tensor_scalar(bit0, dnat, 4, 7, ALU.logical_shift_right, ALU.bitwise_and))
            dve.tensor_copy(bits[:, 0], bit1.rearrange("p (g c) -> p g c", c=HB))
            link(dve.tensor_copy(bits[:, 1], bit0.rearrange("p (g c) -> p g c", c=HB)))
            for v in range(16):
                dve.tensor_scalar(oh1[:, :, v], bits[:, 0], float(v), None, ALU.is_equal)
            for v in range(8):
                ins = dve.tensor_scalar(oh0[:, :, v], bits[:, 1], float(v), None, ALU.is_equal)
            ins.then_inc(oh_hist, 1)
            dve.wait_ge(consts, 3)
            link(dve.tensor_scalar(pint, pidx, 7, None, ALU.bitwise_and))
            link(dve.tensor_copy(cmod, pint))
            link(dve.tensor_scalar(delta[:, :, :], delta[:, :, :], cmod, None, ALU.is_equal))
            link(dve.tensor_scalar(pint, pidx, 0x78, None, ALU.bitwise_and))
            link(dve.tensor_copy(b1off, pint))
            link(dve.tensor_scalar(before, wminus, b1off, None, ALU.is_gt))
            dve.wait_ge(hist_done, 1)
            link(dve.tensor_tensor(masked, ps[MISC][:, 0:HB * 8].rearrange("p (b c) -> p b c", c=HB), delta[:, :, :], ALU.mult))
            link(dve.tensor_reduce(hist, masked, X, ALU.add))
            link(dve.tensor_copy(hist16[:, :, 0], hist))
            dve.tensor_tensor(hist16[:, :, 1], hist, hist16[:, :, 0], ALU.subtract).then_inc(hist_ready, 1)
            statistics(*range(TB))
            norms(0)
            dve.wait_ge(start_done, 1)
            link(dve.tensor_reduce(startf, ps[MISC][:, 64:66], X, ALU.add))
            dve.tensor_scalar(start, startf, float(E - CAP), None, ALU.min).then_inc(start_ready, 1)
            statistics(*range(TB, 2 * TB))

            def edge_keys():
                dve.wait_ge(dst_g, 16)
                dve.wait_ge(iotas, 3)
                link(dve.tensor_scalar(rel, dstw, wbase, None, ALU.subtract))
                link(dve.tensor_scalar(bad, rel, 0.0, None, ALU.is_lt))
                link(dve.scalar_tensor_tensor(bad, rel, float(WIN), bad, ALU.is_ge, ALU.add))
                link(dve.tensor_reduce(badsum, bad, X, ALU.add))
                link(dve.scalar_tensor_tensor(key, bad, FAR, rel, ALU.mult, ALU.add))
                dve.wait_ge(src_g, 16)
                link(dve.tensor_scalar(highi, srcw, 3, 0x7F0, ALU.logical_shift_right, ALU.bitwise_and))
                link(dve.tensor_scalar(lowi, srcw, P - 1, None, ALU.bitwise_and))
                link(dve.tensor_tensor(key, key, highi, ALU.add))
                dve.tensor_copy(low, lowi).then_inc(keys_ready, 1)

            def keys_copy():
                dve.wait_ge(keyT_done, 1)
                for v in range(2):
                    dve.tensor_copy(keyT[:, v, :].rearrange("p (w j) -> p w j", j=CH),
                                    ps[v][:, 0:CH * P].rearrange("p (j w) -> p w j", j=CH)).then_inc(keyT_copied, 1)
                dve.wait_ge(keyT_copied, 2)
                dve.wait_ge(cover_done, 1)
                dve.tensor_scalar(flag, ps[MISC][:, 66:67], float(CAP * P - E), None, ALU.not_equal).then_inc(flag_set, 1)

            for g in range(T):
                if g in SQRT_AT:
                    norms(SQRT_AT[g])
                if g == EDGES_AT:
                    edge_keys()
                for t in T_AFTER.get(g, ()):
                    h_low(t)
                if g == KEYS_AT:
                    keys_copy()
                if g == K + 1:
                    dve.wait_ge(b1_done, 1)
                    link(dve.tensor_reduce(bias1, last[:, :, :], X, ALU.add))
                    dve.wait_ge(b_in, 32)
                    dve.tensor_tensor(bias1, bias1, blin, ALU.add).then_inc(b1_ready, 1)
                if g in STATS_AT:
                    statistics(*STATS_AT[g])
                if g >= 1:
                    weight_max((g - 1) // (2 * K), (g - 1) % (2 * K))
                if g == 4:
                    dve.wait_ge(b_in, 32)
                    dve.tensor_copy(bcol[:, :, :], brel2.unsqueeze(2).to_broadcast([P, K, P])).then_inc(bcol_ready, 1)
                if g == 2 * K:
                    weight_top(0)
                if g == 2 * K + 1:
                    weight_scale(0)
                    dve.tensor_scalar(iS1, iW[0], 1 / SH, None, ALU.mult)
                if g in SPLIT_AT:
                    weight_low(SPLIT_AT[g])
                if g in ONEHOTS_AT:
                    onehots(0, ONEHOTS_AT[g])
            weight_max(1, 2 * K - 1)
            weight_top(1)
            weight_scale(1)

            with dve.Fori(0, T - 1) as i:
                for h in range(2):
                    onehots(i + 1, h)

            slow = dve.value_load(flag[0:1, 0:1], min_val=0, max_val=1)
            with dve.If(slow == 1):
                dve.wait_ge(sl_in, 32)
                dve.tensor_scalar(s_lowi, s_src, P - 1, None, ALU.bitwise_and).then_inc(sl_chain, 1)
                dve.wait_ge(sl_chain, 1)
                dve.tensor_copy(s_low, s_lowi).then_inc(sl_chain, 1)
                dve.tensor_scalar(s_high, s_src, 3, 0x7F0, ALU.logical_shift_right, ALU.bitwise_and).then_inc(sl_chain, 1)
                dve.tensor_copy(s_rel, s_dst).then_inc(sl_chain, 1)
                dve.wait_ge(sl_chain, 4)
                with dve.Fori(0, T) as i:
                    with dve.Fori(0, WT) as u:
                        w = i * WT + u
                        c = 4 + w * 5
                        dve.tensor_scalar(s_tmp, s_rel, 0.0, None, ALU.is_lt).then_inc(sl_chain, 1)
                        dve.wait_ge(sl_chain, c + 1)
                        dve.scalar_tensor_tensor(s_tmp, s_rel, float(WIN), s_tmp, ALU.is_ge, ALU.add).then_inc(sl_chain, 1)
                        dve.wait_ge(sl_chain, c + 2)
                        dve.wait_ge(sl_oh, w * EC + 1)
                        dve.scalar_tensor_tensor(s_key, s_tmp, FAR, s_rel, ALU.mult, ALU.add).then_inc(sl_chain, 1)
                        dve.wait_ge(sl_chain, c + 3)
                        dve.tensor_tensor(s_key, s_key, s_high, ALU.add).then_inc(sl_chain, 1)
                        dve.tensor_scalar(s_rel, s_rel, -float(WIN), None, ALU.add).then_inc(sl_chain, 1)
                        with dve.Fori(0, EC // 2) as m:
                            for h in range(2):
                                dve.wait_ge(sl_chain, c + 5)
                                dve.wait_ge(sl_free, w * EC + 2 * m + h + 1)
                                dve.tensor_scalar(s_oh[h][:, 0:P], iota16[:, 0:P], s_low[:, ds(2 * m + h, 1)], None,
                                                  ALU.is_equal)
                                dve.tensor_scalar(s_oh[h][:, P:OH], iota16[:, :], s_key[:, ds(2 * m + h, 1)], None,
                                                  ALU.is_equal).then_inc(sl_oh, 1)
                        dve.wait_ge(sl_A, w + 1)
                        dve.wait_ge(sl_st, 16 * i + 16)
                        dve.tensor_tensor(A2s[:, :, ds(u * WIN, WIN)],
                                          ps[ACC[0]][:, 0:KEY].rearrange("p (s d) -> p s d", s=HI),
                                          A4[:, ds(i, 1), :, ds(u * WIN, WIN)].rearrange("p o s d -> p (o s) d"),
                                          ALU.subtract).then_inc(sl_A2, 1)

            with dve.Fori(0, B) as b:
                for k in range(K):
                    dve.wait_ge(h1_ready, b * K + k + 1 + K)
                    dve.tensor_reduce(hmax[:, ds(b * K + k, 1)], H1[:, ds(b, 1), k, :].rearrange("p o n -> p (o n)"),
                                      X, ALU.max).then_inc(hmax_part, 1)
            dve.wait_ge(hmax_part, B * K)
            link(dve.tensor_reduce(htop, hmax, X, ALU.max))
            dve.sem_inc(hmax_ready, 1)
            dve.wait_ge(hall_ready, 1)
            exponent(hall, 257, sHs, 3, iH).then_inc(sH_ready, 1)
            dve.wait_ge(sH_ready, 1)
            link(dve.tensor_tensor(iS2, iH, iW[1], ALU.mult))

            def split_low(c, j):
                t = c * -TB + (B * TB + j)
                dve.wait_ge(c_hi, c * TB + j + 1)
                dve.scalar_tensor_tensor(
                    H5[:, ds(t, 1), 1].rearrange("p o k n -> p (o k) n"),
                    H1[:, ds(c * -1 + (B - 1), 1), :, j * P:(j + 1) * P].rearrange("p o k n -> p (o k) n"), sHs,
                    H5[:, ds(t, 1), 0].rearrange("p o k n -> p (o k) n"), ALU.mult, ALU.subtract).then_inc(c_lo, 1)

            def y_low(c, j):
                n = c * -TB + ((B - 1) * TB + j)
                dve.wait_ge(y2_hi, c * TB + j + 1)
                dve.tensor_tensor(Y4[:, ds(n, 1), 1, :].rearrange("p o f -> p (o f)"), ps[GY[j % 2]][:, :],
                                  Y4[:, ds(n, 1), 0, :].rearrange("p o f -> p (o f)"), ALU.subtract).then_inc(y2_lo, 1)

            for j in range(TB):
                split_low(0, j)
            with dve.Fori(0, B - 1) as c:
                for j in range(TB):
                    split_low(c + 1, j)
                    y_low(c, j)
            for j in range(TB):
                y_low(B - 1, j)
            dve.wait_ge(b2_done, 1)
            dve.tensor_copy(bias2[:, :], ps[BIAS][:, :]).then_inc(b2_ready, 1)
            dve.wait_ge(b2_ready, 1)
            with dve.Fori(0, B) as b:
                for j in range(TB):
                    dve.wait_ge(z2_done, b * TB + j + 1)
                    dve.wait_ge(o_out[j % 2], (b * (TB // 2) + j // 2 + 1) * 16)
                    dve.scalar_tensor_tensor(ot[:, j % 2, :], ps[GZ[j]][:, :], iS2, bias2[:, :], ALU.mult, ALU.add)\
                        .then_inc(z2_read, 1)
                    dve.wait_ge(z2_read, b * TB + j + 1 + TB)
                    dve.wait_ge(xr_in[j % 2], (b * (TB // 2) + j // 2 + 1) * 16)
                    dve.scalar_tensor_tensor(ot[:, j % 2, :], ot[:, j % 2, :], 0.0, xb[:, j % 2, :], ALU.max, ALU.add)\
                        .then_inc(o_ready, 1)

        @block.tensor
        def _(pe):
            def transpose_lin(l):
                if l == 1:
                    pe.wait_ge(w_in[1][LIN], 16)
                    pe.wait_ge(start_ready, 1)
                for k in range(K):
                    if l == 0:
                        pe.wait_ge(lin_in[k], 16)
                    for q in range(K):
                        ins = pe.transpose(ps[WTB[l][k]][:, q * P:(q + 1) * P], raw[l][:, LIN, q, k * P:(k + 1) * P], ident[:, :])
                    ins.then_inc(wt_done, 1)

            def fold(g):
                l, t = divmod(g, 2 * K)
                c, q = divmod(t, K)
                if g < K:
                    pe.wait_ge(rel_in[q], 16)
                elif q == 0:
                    pe.wait_ge(w_in[l][c], 16)
                if t == 0:
                    pe.wait_ge(wt_copied, (l + 1) * K)
                if g >= 2:
                    pe.wait_ge(fold_copied, g - 1)
                for k in range(K):
                    ins = pe.matmul(ps[FOLD[t % 2]][:, :], raw[l][:, c, k, q * P:(q + 1) * P], lint[l][:, k, :],
                                    start=(k == 0), stop=(k == K - 1))
                ins.then_inc(fold_done, 1)

            def transpose_h(t):
                pe.wait_ge(h_f32, t + 1)
                if t >= 2:
                    pe.wait_ge(hT_lo, t - 1)
                for k in range(K):
                    ins = pe.transpose(ps[TP[t % 2]][:, k * P:(k + 1) * P], x_of(t)[:, k * P:(k + 1) * P], ident[:, :])
                ins.then_inc(tp_done, 1)

            def split_products(out_, left, right):
                terms = [(k, a, b) for k in range(K) for a, b in ((0, 0), (0, 1), (1, 0))]
                return [(out_, left(k, a), right(k, b)) for k, a, b in terms]

            pe.sem_inc(pair_done, WT // 2)
            pe.sem_inc(y_f32, 1)
            pe.sem_inc(y_lo, 1)
            pe.wait_ge(ident_ready, 1)
            transpose_lin(0)
            for g in range(T):
                if g == HIST_AT:
                    pe.wait_ge(oh_hist, 1)
                    for c in range(EC // HB):
                        ins = pe.matmul(ps[MISC][:, 0:HB * 8], oh1[:, c].rearrange("p v c -> p (v c)"),
                                        oh0[:, c].rearrange("p v c -> p (v c)"), start=(c == 0), stop=(c == EC // HB - 1))
                    ins.then_inc(hist_done, 1)
                if g == START_AT:
                    pe.wait_ge(hist_ready, 1)
                    for b in range(8):
                        ins = pe.matmul(ps[MISC][:, 64:66], before[:, b, :], hist16[:, b, :], start=(b == 0), stop=(b == 7))
                    ins.then_inc(start_done, 1)
                if g == 2 * K - 1:
                    transpose_lin(1)
                fold(g)
                for t in T_AFTER.get(g, ()):
                    transpose_h(t)
                if g == KEYS_AT:
                    pe.wait_ge(keys_ready, 1)
                    for v, rows in enumerate((key, low)):
                        for j in range(CH):
                            ins = pe.transpose(ps[v][:, j * P:(j + 1) * P], rows[:, j * P:(j + 1) * P], ident[:, :])
                    ins.then_inc(keyT_done, 1)
                    pe.matmul(ps[MISC][:, 66:67], ones[:, :], badsum, start=True, stop=True).then_inc(cover_done, 1)

            pe.wait_ge(flag_set, 1)
            slow = pe.value_load(flag[0:1, 0:1], min_val=0, max_val=1)
            pe.wait_ge(w_lo, 1)
            with pe.Fori(0, T) as i:
                pe.wait_ge(hT_lo, i + 1)
                todo = split_products(ps[GY[0]][:, :], lambda k, a: H5[:, ds(i + TB, 1), a, k, :].rearrange("p o n -> p (o n)"),
                                      lambda k, b: Wb[:, 0, 0, b, k, :])
                half = len(todo) // 2
                for u in range(WT):
                    if u == 0:
                        pe.wait_ge(y_f32, i + 1)
                    if u % (WT // 2) == 0:
                        first = u // (WT // 2) * half
                        for n in range(first, first + half):
                            ins = pe.matmul(*todo[n], start=(n == 0), stop=(n == len(todo) - 1))
                        if u > 0:
                            ins.then_inc(y_done, 1)
                    if u % 2 == 0:
                        pe.wait_ge(A_ready, i * (WT // 2) + u // 2 + 1)
                    if u % (WT // 2) == 0:
                        pe.wait_ge(onehot_ready, i * 2 + u // (WT // 2) + 1)
                    for j in range(CH):
                        g, r = divmod(u * CH + j, SIDE)
                        ins = pe.matmul(ps[ACC[u // 2 % 2]][:, u % 2 * KEY:(u % 2 + 1) * KEY], R4[:, g, 0:P, r], R4[:, g, P:OH, r],
                                        start=(j == 0), stop=(j == CH - 1))
                    if u % 2 == 1:
                        ins.then_inc(pair_done, 1)

            with pe.If(slow == 1):
                pe.wait_ge(A_ready, T * WT // 2 + 2)
                pe.sem_inc(sl_free, 2)
                pe.sem_inc(a2_used, 1)
                pe.sem_inc(sl_A2, 1)
                with pe.Fori(0, T * WT) as w:
                    pe.wait_ge(sl_A2, w + 1)

                    def pair(chunk, first, last):
                        for h in range(2):
                            pe.wait_ge(sl_oh, chunk + h + 2)
                            ins = pe.matmul(ps[ACC[0]][:, 0:KEY], s_oh[h][:, 0:P], s_oh[h][:, P:OH],
                                            start=first and h == 0, stop=last and h == 1)
                            ins.then_inc(sl_free, 1)

                    pair(w * EC, True, False)
                    with pe.Fori(1, EC // 2 - 1) as m:
                        pair(w * EC + 2 * m, False, False)
                    pair(w * EC + EC - 2, False, True)
                    pe.wait_ge(sl_free, w * EC + EC + 2)
                    pe.sem_inc(sl_win, 1)
                pe.wait_ge(sl_A2, T * WT + 1)

            with pe.Fori(0, B) as b:
                for q in range(K):
                    z = ps[GZ[q]][:, :].rearrange("p (t n) -> p t n", t=TB)
                    cols = slice(q * P, (q + 1) * P)
                    pe.wait_ge(h1_ready, b * K + q + 1)
                    todo = split_products(z, lambda k, a: Wb[:, 0, 1, a, k, cols], lambda k, c: H5[:, ds(b * TB + TB, TB), c, k, :])
                    for n, (o_, l_, r_) in enumerate(todo):
                        pe.matmul(o_, l_, r_, start=(n == 0), stop=False)
                    pe.wait_ge(y_lo, T + 1)
                    pe.wait_ge(w_lo, 2)
                    pe.wait_ge(A_ready, T * WT // 2 + 2)
                    with pe.If(slow == 1):
                        pe.wait_ge(a2_in, 16 * b + 16)
                        for s in range(HI):
                            for a in range(2):
                                pe.matmul(z, Y4[:, s, a, cols], A2[:, :, s, :], start=False, stop=False)
                    for s in range(HI):
                        for a in range(2):
                            ins = pe.matmul(z, Y4[:, s, a, cols], A4[:, ds(b * TB, TB), s, :],
                                            start=False, stop=(s == HI - 1 and a == 1))
                    ins.then_inc(z1_done, 1)
                with pe.If(slow == 1):
                    pe.drain().then_inc(a2_used, 1)

            pe.wait_ge(bcol_ready, 1)
            pe.wait_ge(brow_in, 16)
            for k in range(K):
                pe.matmul(ps[BIAS][:, :], bcol[:, k, :], lint[1][:, k, :], start=(k == 0), stop=False)
            pe.matmul(ps[BIAS][:, :], ones[0:1, :], brow[0:1, :], start=False, stop=True).then_inc(b2_done, 1)

            pe.wait_ge(w2_lo, 2 * K)
            pe.sem_inc(y2_lo, 2)
            pe.sem_inc(z2_read, TB)
            with pe.Fori(0, B) as c:
                for j in range(TB):
                    pe.wait_ge(c_lo, c * TB + j + 1 + TB)
                    pe.wait_ge(y2_lo, c * TB + j + 1)
                    todo = split_products(ps[GY[j % 2]][:, :],
                                          lambda k, a: H5[:, ds(c * -TB + (B * TB + j), 1), a, k, :].rearrange("p o n -> p (o n)"),
                                          lambda k, b: Wb[:, 1, 0, b, k, :])
                    for n, (o_, l_, r_) in enumerate(todo):
                        ins = pe.matmul(o_, l_, r_, start=(n == 0), stop=(n == len(todo) - 1))
                    ins.then_inc(y2_done, 1)

            with pe.Fori(0, B) as b:
                for j in range(TB):
                    z = ps[GZ[j]][:, :]
                    pe.wait_ge(z2_read, b * TB + j + 1)
                    todo = split_products(z, lambda k, a: H5[:, ds((b + 1) * TB + j, 1), a, k, :].rearrange("p o n -> p (o n)"),
                                          lambda k, c: Wb[:, 1, 1, c, k, :])
                    for n, (o_, l_, r_) in enumerate(todo):
                        pe.matmul(o_, l_, r_, start=(n == 0), stop=False)
                    pe.wait_ge(y2_lo, T + 2)
                    with pe.If(slow == 1):
                        pe.wait_ge(a2_in, 16 * b + 16 * B + 16)
                        for s in range(HI):
                            for a in range(2):
                                pe.matmul(z, A2[:, j, s, :], Y4[:, s, a, :], start=False, stop=False)
                    for s in range(HI):
                        for a in range(2):
                            ins = pe.matmul(z, A4[:, ds(b * TB + j, 1), s, :].rearrange("p o n -> p (o n)"), Y4[:, s, a, :],
                                            start=False, stop=(s == HI - 1 and a == 1))
                    ins.then_inc(z2_done, 1)
                with pe.If(slow == 1):
                    pe.drain().then_inc(a2_used, 1)


_INS = ["x", "src", "dst"] + [f"L0_gnn_{n}" for n in ("W_rel1", "b_rel1", "W_root1", "W_lin1", "b_lin1",
                                                     "W_rel2", "b_rel2", "W_root2", "W_lin2", "b_lin2")]


def kernel(**inputs):
    import numpy as _np
    import concourse.bacc as _bacc
    from concourse import mybir as _mybir
    from concourse.bass_utils import run_bass_kernel_spmd as _run

    nc = _bacc.Bacc("TRN2", target_bir_lowering=False, num_devices=1)
    arrays, args = {}, []
    for name in _INS:
        a = _np.ascontiguousarray(inputs[name])
        arrays[f"in_{name}"] = a
        args.append(nc.dram_tensor(f"in_{name}", a.shape, _mybir.dt.from_np(a.dtype), kind="ExternalInput").ap())
    out = nc.dram_tensor("out_0", inputs["x"].shape, _mybir.dt.float32, kind="ExternalOutput").ap()
    gnn_block_kernel(nc, *args, out)
    return _run(nc, [arrays], core_ids=[0]).results[0]["out_0"]
```
